# Optimizing a Trainium2 kernel written in Bass

```python
import numpy as np
import jax
import jax.numpy as jnp

def _softmax(x, axis=-1):
    return jax.nn.softmax(x, axis=axis)

def _gelu(x):
    return jax.nn.gelu(x, approximate=True)

def _silu(x):
    return jax.nn.silu(x)

def _sigmoid(x):
    return jax.nn.sigmoid(x)

def _layernorm(x, axis=-1, eps=1e-05):
    m = jnp.mean(x, axis=axis, keepdims=True)
    v = jnp.var(x, axis=axis, keepdims=True)
    return (x - m) / jnp.sqrt(v + eps)

def _scatter_add(tgt, idx, src, axis=0):
    return tgt.at[idx].add(src)

def _segment_sum(src, seg, n):
    return jax.ops.segment_sum(src, seg, n)
kernel_name = 'mk_dlrm_tower_d1_rec_r8_ef890d'

def setup_inputs(seed: int=0):
    np.random.seed(seed)
    _w = jnp.asarray

    def _rec_inputs():
        import jax
        import jax.numpy as jnp
        _tk = jax.random.key(seed)
        dense_ctx = jax.random.normal(jax.random.fold_in(_tk, 190), (2048, 16), jnp.float32)
        ids = jnp.stack([jax.random.randint(jax.random.fold_in(_tk, 200 + f), (2048,), 0, v, jnp.int32) for f, v in enumerate([12500, 12500, 12500, 125000, 1250, 1250, 125000, 12500, 1250, 1250, 125000, 1250, 1250, 1000, 12500, 1000, 1000, 125000, 1000, 12500, 1000, 1000, 12500, 1000, 12500, 1000, 1250, 125000, 12500, 12500, 1000, 12500, 12500, 1000, 12500, 125000, 1000, 1250, 1250, 12500])], axis=1)
        tbl_0 = 0.05 * jax.random.normal(jax.random.fold_in(_tk, 500 + 0), (12500, 32), jnp.float32)
        tbl_1 = 0.05 * jax.random.normal(jax.random.fold_in(_tk, 500 + 1), (12500, 32), jnp.float32)
        tbl_2 = 0.05 * jax.random.normal(jax.random.fold_in(_tk, 500 + 2), (12500, 32), jnp.float32)
        tbl_3 = 0.05 * jax.random.normal(jax.random.fold_in(_tk, 500 + 3), (125000, 32), jnp.float32)
        tbl_4 = 0.05 * jax.random.normal(jax.random.fold_in(_tk, 500 + 4), (1250, 32), jnp.float32)
        tbl_5 = 0.05 * jax.random.normal(jax.random.fold_in(_tk, 500 + 5), (1250, 32), jnp.float32)
        tbl_6 = 0.05 * jax.random.normal(jax.random.fold_in(_tk, 500 + 6), (125000, 32), jnp.float32)
        tbl_7 = 0.05 * jax.random.normal(jax.random.fold_in(_tk, 500 + 7), (12500, 32), jnp.float32)
        tbl_8 = 0.05 * jax.random.normal(jax.random.fold_in(_tk, 500 + 8), (1250, 32), jnp.float32)
        tbl_9 = 0.05 * jax.random.normal(jax.random.fold_in(_tk, 500 + 9), (1250, 32), jnp.float32)
        tbl_10 = 0.05 * jax.random.normal(jax.random.fold_in(_tk, 500 + 10), (125000, 32), jnp.float32)
        tbl_11 = 0.05 * jax.random.normal(jax.random.fold_in(_tk, 500 + 11), (1250, 32), jnp.float32)
        tbl_12 = 0.05 * jax.random.normal(jax.random.fold_in(_tk, 500 + 12), (1250, 32), jnp.float32)
        tbl_13 = 0.05 * jax.random.normal(jax.random.fold_in(_tk, 500 + 13), (1000, 32), jnp.float32)
        tbl_14 = 0.05 * jax.random.normal(jax.random.fold_in(_tk, 500 + 14), (12500, 32), jnp.float32)
        tbl_15 = 0.05 * jax.random.normal(jax.random.fold_in(_tk, 500 + 15), (1000, 32), jnp.float32)
        tbl_16 = 0.05 * jax.random.normal(jax.random.fold_in(_tk, 500 + 16), (1000, 32), jnp.float32)
        tbl_17 = 0.05 * jax.random.normal(jax.random.fold_in(_tk, 500 + 17), (125000, 32), jnp.float32)
        tbl_18 = 0.05 * jax.random.normal(jax.random.fold_in(_tk, 500 + 18), (1000, 32), jnp.float32)
        tbl_19 = 0.05 * jax.random.normal(jax.random.fold_in(_tk, 500 + 19), (12500, 32), jnp.float32)
        tbl_20 = 0.05 * jax.random.normal(jax.random.fold_in(_tk, 500 + 20), (1000, 32), jnp.float32)
        tbl_21 = 0.05 * jax.random.normal(jax.random.fold_in(_tk, 500 + 21), (1000, 32), jnp.float32)
        tbl_22 = 0.05 * jax.random.normal(jax.random.fold_in(_tk, 500 + 22), (12500, 32), jnp.float32)
        tbl_23 = 0.05 * jax.random.normal(jax.random.fold_in(_tk, 500 + 23), (1000, 32), jnp.float32)
        tbl_24 = 0.05 * jax.random.normal(jax.random.fold_in(_tk, 500 + 24), (12500, 32), jnp.float32)
        tbl_25 = 0.05 * jax.random.normal(jax.random.fold_in(_tk, 500 + 25), (1000, 32), jnp.float32)
        tbl_26 = 0.05 * jax.random.normal(jax.random.fold_in(_tk, 500 + 26), (1250, 32), jnp.float32)
        tbl_27 = 0.05 * jax.random.normal(jax.random.fold_in(_tk, 500 + 27), (125000, 32), jnp.float32)
        tbl_28 = 0.05 * jax.random.normal(jax.random.fold_in(_tk, 500 + 28), (12500, 32), jnp.float32)
        tbl_29 = 0.05 * jax.random.normal(jax.random.fold_in(_tk, 500 + 29), (12500, 32), jnp.float32)
        tbl_30 = 0.05 * jax.random.normal(jax.random.fold_in(_tk, 500 + 30), (1000, 32), jnp.float32)
        tbl_31 = 0.05 * jax.random.normal(jax.random.fold_in(_tk, 500 + 31), (12500, 32), jnp.float32)
        tbl_32 = 0.05 * jax.random.normal(jax.random.fold_in(_tk, 500 + 32), (12500, 32), jnp.float32)
        tbl_33 = 0.05 * jax.random.normal(jax.random.fold_in(_tk, 500 + 33), (1000, 32), jnp.float32)
        tbl_34 = 0.05 * jax.random.normal(jax.random.fold_in(_tk, 500 + 34), (12500, 32), jnp.float32)
        tbl_35 = 0.05 * jax.random.normal(jax.random.fold_in(_tk, 500 + 35), (125000, 32), jnp.float32)
        tbl_36 = 0.05 * jax.random.normal(jax.random.fold_in(_tk, 500 + 36), (1000, 32), jnp.float32)
        tbl_37 = 0.05 * jax.random.normal(jax.random.fold_in(_tk, 500 + 37), (1250, 32), jnp.float32)
        tbl_38 = 0.05 * jax.random.normal(jax.random.fold_in(_tk, 500 + 38), (1250, 32), jnp.float32)
        tbl_39 = 0.05 * jax.random.normal(jax.random.fold_in(_tk, 500 + 39), (12500, 32), jnp.float32)
        _rk = jax.random.fold_in(_tk, 7)
        W_top1 = 0.0354441 * jax.random.normal(jax.random.fold_in(_tk, 801), (796, 512), jnp.float32)
        W_top2 = 0.0441942 * jax.random.normal(jax.random.fold_in(_tk, 802), (512, 256), jnp.float32)
        W_top3 = 0.0625 * jax.random.normal(jax.random.fold_in(_tk, 803), (256, 1), jnp.float32)
        b_top1 = jnp.zeros((512,), jnp.float32)
        b_top2 = jnp.zeros((256,), jnp.float32)
        return (dense_ctx, ids, tbl_0, tbl_1, tbl_2, tbl_3, tbl_4, tbl_5, tbl_6, tbl_7, tbl_8, tbl_9, tbl_10, tbl_11, tbl_12, tbl_13, tbl_14, tbl_15, tbl_16, tbl_17, tbl_18, tbl_19, tbl_20, tbl_21, tbl_22, tbl_23, tbl_24, tbl_25, tbl_26, tbl_27, tbl_28, tbl_29, tbl_30, tbl_31, tbl_32, tbl_33, tbl_34, tbl_35, tbl_36, tbl_37, tbl_38, tbl_39, W_top1, b_top1, W_top2, b_top2, W_top3)
    dense_ctx, ids, tbl_0, tbl_1, tbl_2, tbl_3, tbl_4, tbl_5, tbl_6, tbl_7, tbl_8, tbl_9, tbl_10, tbl_11, tbl_12, tbl_13, tbl_14, tbl_15, tbl_16, tbl_17, tbl_18, tbl_19, tbl_20, tbl_21, tbl_22, tbl_23, tbl_24, tbl_25, tbl_26, tbl_27, tbl_28, tbl_29, tbl_30, tbl_31, tbl_32, tbl_33, tbl_34, tbl_35, tbl_36, tbl_37, tbl_38, tbl_39, W_top1, b_top1, W_top2, b_top2, W_top3 = _rec_inputs()

    def _L0_rec_setup():
        import jax, jax.numpy as jnp
        import numpy as np
        NUM_FIELDS = 40
        EMBED_DIM = 32
        BATCH = 512
        NUM_PAIRS = NUM_FIELDS * (NUM_FIELDS - 1) // 2
        key = jax.random.key(seed)
        k1, k2 = jax.random.split(key)
        inputs = jax.random.normal(k1, (BATCH, NUM_FIELDS, EMBED_DIM), dtype=jnp.float32)
        std = (2.0 / (EMBED_DIM + EMBED_DIM)) ** 0.5
        bilinear_matrices = jax.random.normal(k2, (NUM_PAIRS, EMBED_DIM, EMBED_DIM), dtype=jnp.float32) * std
        return {'inputs': inputs, 'bilinear_matrices': bilinear_matrices}
    _L0_rec_all = _L0_rec_setup()
    _L0_rec_in = {k: v for k, v in _L0_rec_all.items() if k in ('bilinear_matrices',)}
    del _L0_rec_all
    return {'dense_ctx': dense_ctx, 'ids': ids, 'tbl_0': tbl_0, 'tbl_1': tbl_1, 'tbl_2': tbl_2, 'tbl_3': tbl_3, 'tbl_4': tbl_4, 'tbl_5': tbl_5, 'tbl_6': tbl_6, 'tbl_7': tbl_7, 'tbl_8': tbl_8, 'tbl_9': tbl_9, 'tbl_10': tbl_10, 'tbl_11': tbl_11, 'tbl_12': tbl_12, 'tbl_13': tbl_13, 'tbl_14': tbl_14, 'tbl_15': tbl_15, 'tbl_16': tbl_16, 'tbl_17': tbl_17, 'tbl_18': tbl_18, 'tbl_19': tbl_19, 'tbl_20': tbl_20, 'tbl_21': tbl_21, 'tbl_22': tbl_22, 'tbl_23': tbl_23, 'tbl_24': tbl_24, 'tbl_25': tbl_25, 'tbl_26': tbl_26, 'tbl_27': tbl_27, 'tbl_28': tbl_28, 'tbl_29': tbl_29, 'tbl_30': tbl_30, 'tbl_31': tbl_31, 'tbl_32': tbl_32, 'tbl_33': tbl_33, 'tbl_34': tbl_34, 'tbl_35': tbl_35, 'tbl_36': tbl_36, 'tbl_37': tbl_37, 'tbl_38': tbl_38, 'tbl_39': tbl_39, 'W_top1': W_top1, 'b_top1': b_top1, 'W_top2': W_top2, 'b_top2': b_top2, 'W_top3': W_top3, 'L0_rec_bilinear_matrices': _L0_rec_in['bilinear_matrices']}

def reference(dense_ctx, ids, tbl_0, tbl_1, tbl_2, tbl_3, tbl_4, tbl_5, tbl_6, tbl_7, tbl_8, tbl_9, tbl_10, tbl_11, tbl_12, tbl_13, tbl_14, tbl_15, tbl_16, tbl_17, tbl_18, tbl_19, tbl_20, tbl_21, tbl_22, tbl_23, tbl_24, tbl_25, tbl_26, tbl_27, tbl_28, tbl_29, tbl_30, tbl_31, tbl_32, tbl_33, tbl_34, tbl_35, tbl_36, tbl_37, tbl_38, tbl_39, W_top1, b_top1, W_top2, b_top2, W_top3, L0_rec_bilinear_matrices):
    import jax
    import jax.numpy as jnp

    def _L0_rec_ref(inputs, bilinear_matrices):
        import jax, jax.numpy as jnp
        import numpy as np
        NUM_FIELDS = 40
        EMBED_DIM = 32
        BATCH = 512
        NUM_PAIRS = NUM_FIELDS * (NUM_FIELDS - 1) // 2
        num_fields = inputs.shape[1]
        iidx, jidx = jnp.triu_indices(num_fields, k=1)
        xi = inputs[:, iidx, :]
        xj = inputs[:, jidx, :]
        out = jnp.einsum('bpd,pde,bpe->bp', xi, bilinear_matrices, xj)
        return out
    e = jnp.stack([tbl_0[ids[:, 0]], tbl_1[ids[:, 1]], tbl_2[ids[:, 2]], tbl_3[ids[:, 3]], tbl_4[ids[:, 4]], tbl_5[ids[:, 5]], tbl_6[ids[:, 6]], tbl_7[ids[:, 7]], tbl_8[ids[:, 8]], tbl_9[ids[:, 9]], tbl_10[ids[:, 10]], tbl_11[ids[:, 11]], tbl_12[ids[:, 12]], tbl_13[ids[:, 13]], tbl_14[ids[:, 14]], tbl_15[ids[:, 15]], tbl_16[ids[:, 16]], tbl_17[ids[:, 17]], tbl_18[ids[:, 18]], tbl_19[ids[:, 19]], tbl_20[ids[:, 20]], tbl_21[ids[:, 21]], tbl_22[ids[:, 22]], tbl_23[ids[:, 23]], tbl_24[ids[:, 24]], tbl_25[ids[:, 25]], tbl_26[ids[:, 26]], tbl_27[ids[:, 27]], tbl_28[ids[:, 28]], tbl_29[ids[:, 29]], tbl_30[ids[:, 30]], tbl_31[ids[:, 31]], tbl_32[ids[:, 32]], tbl_33[ids[:, 33]], tbl_34[ids[:, 34]], tbl_35[ids[:, 35]], tbl_36[ids[:, 36]], tbl_37[ids[:, 37]], tbl_38[ids[:, 38]], tbl_39[ids[:, 39]]], axis=1)
    z = _L0_rec_ref(e, L0_rec_bilinear_matrices)
    z = z.reshape(z.shape[0], -1)
    h = jnp.concatenate([z, dense_ctx], axis=1)
    h = jnp.maximum(h @ W_top1 + b_top1, 0.0)
    h = jnp.maximum(h @ W_top2 + b_top2, 0.0)
    y = h @ W_top3
    return y

_drawn_inputs = setup_inputs


def setup_inputs(seed=0):
    import zlib

    import numpy as np

    out = dict(_drawn_inputs(seed))
    spreads = {'b_top1': (0.0, 0.1), 'b_top2': (0.0, 0.1)}
    factors = {'tbl_0': 3.61,
     'tbl_1': 3.386,
     'tbl_2': 3.526,
     'tbl_3': 2.959,
     'tbl_4': 3.321,
     'tbl_5': 3.053,
     'tbl_6': 3.507,
     'tbl_7': 3.286,
     'tbl_8': 3.058,
     'tbl_9': 2.919,
     'tbl_10': 3.248,
     'tbl_11': 3.709,
     'tbl_12': 2.937,
     'tbl_13': 3.263,
     'tbl_14': 3.271,
     'tbl_15': 3.343,
     'tbl_16': 3.243,
     'tbl_17': 3.098,
     'tbl_18': 3.487,
     'tbl_19': 3.305,
     'tbl_20': 3.114,
     'tbl_21': 3.394,
     'tbl_22': 3.265,
     'tbl_23': 2.93,
     'tbl_24': 3.34,
     'tbl_25': 3.438,
     'tbl_26': 3.048,
     'tbl_27': 3.448,
     'tbl_28': 3.141,
     'tbl_29': 3.269,
     'tbl_30': 3.333,
     'tbl_31': 2.957,
     'tbl_32': 3.35,
     'tbl_33': 3.215,
     'tbl_34': 3.229,
     'tbl_35': 3.202,
     'tbl_36': 3.547,
     'tbl_37': 3.339,
     'tbl_38': 3.284,
     'tbl_39': 3.098}
    for name, (base, spread) in spreads.items():
        noise = np.random.default_rng([zlib.crc32(name.encode()), seed]).standard_normal(out[name].shape)
        drawn = base * np.exp(spread * noise) if base else spread * noise
        out[name] = jnp.asarray(drawn.astype(out[name].dtype))
    for name, factor in factors.items():
        out[name] = (out[name] * factor).astype(out[name].dtype)
    return out
```

```python
from contextlib import ExitStack

import concourse.bass as bass
from concourse import mybir

F32, BF16, I32 = mybir.dt.float32, mybir.dt.bfloat16, mybir.dt.int32
ALU, ACT = mybir.AluOpType, mybir.ActivationFunctionType

P = 128
BATCH, FIELDS, D, DENSE = 2048, 40, 32, 16
HID1, HID2 = 512, 256
BLK = 256
NB = BATCH // BLK
BT = BLK // P
GF = P // D
NG = FIELDS // GF
DMA = 16


def plan():
    units = []
    for G in range(NG):
        for a in range(G):
            units.append((G, [GF * a + k for k in range(GF)]))
        units.append((G, [GF * G + k for k in range(GF - 1)]))
    G, fields = units[0]
    if len(units) % 2:
        units[0:1] = [(G, fields[:2]), (G, fields[2:])]
    return units


UNITS = plan()
NU = len(UNITS)
FIRST_CHUNK = [sum(len(f) for _, f in UNITS[:u]) for u in range(NU + 1)]
CHUNKS = FIRST_CHUNK[NU]
LAST_UNIT_OF = [max(u for u in range(NU) if UNITS[u][0] == G) for G in range(NG)]
FIRST_UNIT_OF = [min(u for u in range(NU) if UNITS[u][0] == G) for G in range(NG)]
LAST_USE_OF = [max(u for u in range(NU) if UNITS[u][1][0] // GF == g) for g in range(NG)]

SPAN = 8
ZCH = 4 * SPAN
ZT = -(-CHUNKS // ZCH)
H1T, H2T = HID1 // P, HID2 // P
HJ = H1T + H2T + 1

PIECE = 8
NP = -(-CHUNKS // PIECE)
RING = 5
LAPS = NG // RING

AHEAD = 4
TURN_AT = {g: FIRST_UNIT_OF[NG - 1] + 1 + 2 * g for g in range(AHEAD)}
TURN_AT |= {4: 3, 5: 7, 6: 12, 7: 18, 8: 25, 9: 33}
TURN_FIRST = {g: FIRST_UNIT_OF[g] - 2 for g in range(AHEAD, NG)}
PRE = 3
MLP_AT = [2, 3, 4, 5, 6, 7, 8]


def place(c):
    tile, r = divmod(c, ZCH)
    q, o = r % 4, r // 4
    return tile, q, o, o == 0, (o == SPAN - 1 or c + 4 >= CHUNKS)


def turns_in(first, last):
    out = {}
    for g in range(AHEAD, NG):
        out[(TURN_FIRST if first else TURN_AT)[g]] = (g, 0)
    if not last:
        for g in range(AHEAD):
            out[TURN_AT[g]] = (g, 1)
    return out


def tower(nc, ids, dense, tables, m_rows, w1, b1, w2, b2, w3, out):
    ctx = ExitStack()
    with ctx:
        def sb(name, shape, dt):
            return ctx.enter_context(nc.sbuf_tensor(name, shape, dt))

        def sem(name):
            return ctx.enter_context(nc.semaphore(name))

        ident = sb("ident", [P, P], F32)
        identb = sb("identb", [P, P], BF16)
        sel = sb("sel", [P, GF * (SPAN - 1) + 32], F32)
        pass1 = sb("pass1", [P, CHUNKS, P], BF16)
        pass2 = sb("pass2", [P, CHUNKS, P], BF16)
        m_in = sb("m_in", [P, 2, PIECE * P], F32)
        w1_sb = sb("w1_sb", [P, ZT, HID1], F32)
        w2_sb = sb("w2_sb", [P, H1T, HID2], F32)
        w3_sb = sb("w3_sb", [P, H2T], F32)
        b1_sb = sb("b1_sb", [P, H1T], F32)
        b2_sb = sb("b2_sb", [P, H2T], F32)
        idx_first = sb("idx_first", [P, BT, FIELDS], I32)
        idx = sb("idx", [P, LAPS, BT, FIELDS // LAPS], I32)
        rows = sb("rows", [P, RING, BT, P], F32)
        rest = sb("rest", [P, 2, BT, P], F32)
        parts = sb("parts", [P, 2, BT * GF, 4, D], BF16)
        xparts = sb("xparts", [P, FIELDS, BLK], BF16)
        xcols = sb("xcols", [P, NG, BLK], F32)
        prod = sb("prod", [P, 2, GF, BLK], F32)
        dpad = sb("dpad", [P, BT, 32], F32)
        z = sb("z", [P, ZT, BLK], F32)
        h1 = sb("h1", [P, H1T, BLK], F32)
        h2 = sb("h2", [P, H2T, BLK], F32)
        y = sb("y", [1, BLK], F32)
        Y = [ctx.enter_context(nc.psum_tensor(f"Y{k}", [P, GF, BLK], F32)) for k in range(2)]
        Z = [ctx.enter_context(nc.psum_tensor(f"Z{k}", [P, 512], F32)) for k in range(2)]
        turn = ctx.enter_context(nc.psum_tensor("turn", [P, 512], F32))
        H = ctx.enter_context(nc.psum_tensor("H", [P, 512], F32))
        turnb = turn[:, :].bitcast(BF16)

        s_zero = sem("s_zero")
        s_const = sem("s_const")
        s_idx_first = sem("s_idx_first")
        s_idx = [sem(f"s_idx{k}") for k in range(LAPS)]
        s_begun = sem("s_begun")
        s_rows = [sem(f"s_rows{k}") for k in range(RING)]
        s_hi = sem("s_hi")
        s_rest = sem("s_rest")
        s_mid = sem("s_mid")
        s_parts = sem("s_parts")
        s_turned = sem("s_turned")
        s_cols = sem("s_cols")
        s_y = sem("s_y")
        s_prod = sem("s_prod")
        s_z = sem("s_z")
        s_zs = sem("s_zs")
        s_h = sem("s_h")
        s_hs = sem("s_hs")
        s_min = [sem(f"s_min{k}") for k in range(2)]
        s_mh = sem("s_mh")
        s_mr = sem("s_mr")
        s_mm = sem("s_mm")
        s_m = sem("s_m")
        s_w = sem("s_w")
        s_dense = sem("s_dense")
        s_out = sem("s_out")

        block = ctx.enter_context(nc.Block())

        def some(value):
            return not isinstance(value, int) or value > 0

        def rows_by(n, g):
            return (n * LAPS + g // RING + 1) * GF * BT * DMA

        def pieces_by(u):
            return -(-FIRST_CHUNK[min(u, NU - 1) + 1] // PIECE)

        def piece(p):
            lo, hi = PIECE * p, min(PIECE * (p + 1), CHUNKS)
            return (pass1[:, lo:hi, :].rearrange("p c n -> p (c n)"), pass2[:, lo:hi, :].rearrange("p c n -> p (c n)"),
                    m_in[:, p % 2, 0:(hi - lo) * P])

        def pieces_at(u):
            done = pieces_by(AHEAD_PIECES + u - 1) if u >= 0 else 0
            return range(done, pieces_by(AHEAD_PIECES + u))

        AHEAD_PIECES = 4

        @block.sync
        def _(sp):
            def load_idx(n, lap):
                if not isinstance(n, int):
                    for k in range(RING):
                        sp.wait_ge(s_rows[k], rows_by(n - 1, lap * RING + k))
                w = FIELDS // LAPS
                src = ids.rearrange("(n t p) f -> p n t f", t=BT, p=P)
                if isinstance(n, int):
                    src = src[:, n, :, lap * w:(lap + 1) * w]
                else:
                    src = src[:, bass.ds(n, 1), :, lap * w:(lap + 1) * w].rearrange("p n t f -> p (n t) f")
                sp.dma_start(idx[:, lap, :, :], src).then_inc(s_idx[lap], DMA)

            def load_dense(n):
                if some(n * ZT):
                    sp.wait_ge(s_z, n * ZT)
                src = dense.rearrange("(n t p) f -> p n t f", t=BT, p=P)
                if isinstance(n, int):
                    src = src[:, n, :, :]
                else:
                    src = src[:, bass.ds(n, 1), :, :].rearrange("p n t f -> p (n t) f")
                sp.dma_start(dpad[:, :, 32 - DENSE:32], src).then_inc(s_dense, DMA)

            def store(n):
                sp.wait_ge(s_hs, (n + 1) * HJ)
                dst = out.rearrange("(n b) o -> n (b o)", b=BLK)
                if isinstance(n, int):
                    dst = dst[n:n + 1, :]
                else:
                    dst = dst[bass.ds(n, 1), :]
                sp.dma_start(dst, y[:, :]).then_inc(s_out, DMA)

            sp.dma_start(idx_first[:, :, :], ids[0:BLK, :].rearrange("(t p) f -> p t f", p=P)).then_inc(s_idx_first, DMA)
            for lap in range(LAPS):
                load_idx(1, lap)
            sp.wait_ge(s_const, 1)
            for p in range(NP):
                if p >= 2:
                    sp.wait_ge(s_m, p - 1)
                lo, hi = PIECE * P * p, min(PIECE * (p + 1), CHUNKS) * P
                for q in range(4):
                    sp.dma_start(m_in[D * q:D * (q + 1), p % 2, 0:hi - lo], m_rows[:, lo:hi])\
                      .then_inc(s_min[p % 2], DMA)
                if p == 2:
                    load_dense(0)
                if p == 8:
                    sp.dma_start(w1_sb[:, :, :], w1.rearrange("(t p) n -> p t n", p=P)).then_inc(s_w, DMA)
                    sp.dma_start(w2_sb[:, :, :], w2.rearrange("(t p) n -> p t n", p=P)).then_inc(s_w, DMA)
                    sp.dma_start(w3_sb[:, :], w3).then_inc(s_w, DMA)
                    sp.dma_start(b1_sb[:, :], b1).then_inc(s_w, DMA)
                    sp.dma_start(b2_sb[:, :], b2).then_inc(s_w, DMA)
            load_dense(1)
            with sp.Fori(0, NB - 2) as n:
                load_idx(n + 2, 0)
                store(n)
                load_idx(n + 2, 1)
                load_dense(n + 2)
            store(NB - 2)
            store(NB - 1)
            sp.wait_ge(s_out, NB * DMA)

        @block.gpsimd
        def _(pool):
            pool.memset(ident[:, :], 0.0).then_inc(s_zero, 1)
            pool.memset(identb[:, :], 0.0).then_inc(s_zero, 1)
            pool.memset(sel[:, :], 0.0).then_inc(s_zero, 1)
            pool.memset(dpad[:, :, 0:32 - DENSE], 0.0).then_inc(s_zero, 1)
            pool.wait_ge(s_zero, 4)
            for m in (ident, identb):
                pool.affine_select(out=m[:, :], in_=m[:, :], compare_op=ALU.not_equal, fill=1.0, base=0,
                                   pattern=[[-1, P]], channel_multiplier=1).then_inc(s_zero, 1)
            for s in range(GF):
                c = GF * (SPAN - 1) + s
                pool.wait_ge(s_zero, 6 + s)
                pool.memset(sel[D * s:D * (s + 1), c:c + 1], 1.0).then_inc(s_zero, 1)
            pool.wait_ge(s_zero, 6 + GF)
            pool.engine_nop().then_inc(s_const, 1)

            def gather(n):
                for lap in range(LAPS):
                    if isinstance(n, int):
                        pool.wait_ge(s_idx_first, DMA)
                    else:
                        pool.wait_ge(s_idx[lap], n * DMA)
                    for k in range(RING):
                        g = lap * RING + k
                        if some(2 * (n * NG + g - RING + 1)):
                            pool.wait_ge(s_turned, 2 * (n * NG + g - RING + 1))
                        pool.sem_inc(s_begun, 1)
                        for f in range(GF):
                            for t in range(BT):
                                at = GF * g + f if isinstance(n, int) else GF * k + f
                                which = idx_first[:, t, at:at + 1] if isinstance(n, int) else idx[:, lap, t, at:at + 1]
                                pool.indirect_dma_start(
                                    out=rows[:, k, t, D * f:D * (f + 1)], out_offset=None,
                                    in_=tables[GF * g + f],
                                    in_offset=bass.IndirectOffsetOnAxis(ap=which, axis=0),
                                ).then_inc(s_rows[k], DMA)

            gather(0)
            with pool.Fori(1, NB) as n:
                gather(n)

        @block.tensor
        def _(pe):
            def multiply(n, u, first):
                G, fields = UNITS[u]
                if some(n * NU + u - 1):
                    pe.wait_ge(s_prod, n * NU + u - 1)
                pe.wait_ge(s_cols, 2 * (n * NG + fields[0] // GF) + 1)
                if first:
                    pe.wait_ge(s_m, pieces_by(u))
                for k, i in enumerate(fields):
                    c = FIRST_CHUNK[u] + k
                    pe.matmul(Y[u % 2][:, k, :], pass1[:, c, :], xparts[:, i, :], start=True, stop=False)
                    last = pe.matmul(Y[u % 2][:, k, :], pass2[0:96, c, :], xparts[0:96, i, :],
                                     start=False, stop=True)
                last.then_inc(s_y, 1)

            def add_up(n, u):
                pe.wait_ge(s_prod, n * NU + u + 1)
                for k in range(len(UNITS[u][1])):
                    c = FIRST_CHUNK[u] + k
                    tile, q, o, start, stop = place(c)
                    final = tile == ZT - 1
                    bank = H if final else Z[tile % 2]
                    if c == ZCH * tile:
                        if final:
                            if some(n * HJ):
                                pe.wait_ge(s_hs, n * HJ)
                        elif tile < 2:
                            if some(n * ZT - ZT + tile + 5):
                                pe.wait_ge(s_zs, n * ZT - ZT + tile + 5)
                        else:
                            pe.wait_ge(s_zs, n * ZT + tile - 1)
                    last = pe.matmul(bank[32 * q:32 * q + 32, 0:BLK],
                                     sel[:, GF * (SPAN - 1 - o):GF * (SPAN - 1 - o) + 32],
                                     prod[:, u % 2, k, :], start=start, stop=stop)
                    if c % ZCH == ZCH - 1 or c == CHUNKS - 1:
                        last.then_inc(s_z, 1)
                    if final and q == 3 and start:
                        pe.wait_ge(s_dense, (n + 1) * DMA)
                        for t in range(BT):
                            pe.matmul(H[96:P, t * P:(t + 1) * P], dpad[:, t, :], ident[:, :],
                                      start=False, stop=False, skip_group_check=True)

            def turn_parts(n, g):
                gg = n * NG + g
                if some(2 * gg):
                    pe.wait_ge(s_cols, 2 * gg)
                pe.wait_ge(s_parts, gg + 1)
                for f in range(GF):
                    for t in range(BT):
                        last = pe.transpose(turnb[:, f * BLK + t * P:f * BLK + (t + 1) * P],
                                            parts[:, g % 2, t * GF + f, :, :].rearrange("p a d -> p (a d)"),
                                            identb[:, :])
                last.then_inc(s_turned, 1)

            def turn_rows(n, g):
                pe.wait_ge(s_cols, 2 * (n * NG + g) + 1)
                for t in range(BT):
                    last = pe.transpose(turn[:, t * P:(t + 1) * P], rows[:, g % RING, t, :], ident[:, :])
                last.then_inc(s_turned, 1)

            def mlp(n, j):
                if j == 0:
                    pe.wait_ge(s_zs, (n + 1) * ZT)
                else:
                    pe.wait_ge(s_hs, n * HJ + j)
                if j < H1T:
                    steps = [(w1_sb[:, k, j * P:(j + 1) * P], z[:, k, :]) for k in range(ZT)]
                elif j < H1T + H2T:
                    m = j - H1T
                    steps = [(w2_sb[:, k, m * P:(m + 1) * P], h1[:, k, :]) for k in range(H1T)]
                else:
                    steps = [(w3_sb[:, k:k + 1], h2[:, k, :]) for k in range(H2T)]
                for k, (w, x) in enumerate(steps):
                    last = pe.matmul(H[0:w.shape[1], 0:BLK], w, x, start=k == 0, stop=k == len(steps) - 1)
                last.then_inc(s_h, 1)

            def one_block(n, first, last):
                turns = turns_in(first, last)
                for u in range(NU):
                    multiply(n, u, first)
                    if u:
                        add_up(n, u - 1)
                    elif not first:
                        add_up(n - 1, NU - 1)
                    if u in turns:
                        g, ahead = turns[u]
                        turn_parts(n + ahead, g)
                    if u - 1 in turns:
                        g, ahead = turns[u - 1]
                        turn_rows(n + ahead, g)
                    if u in MLP_AT and not first:
                        mlp(n - 1, MLP_AT.index(u))

            pe.wait_ge(s_const, 1)
            for g in range(AHEAD):
                turn_parts(0, g)
                turn_rows(0, g)
            one_block(0, True, False)
            pe.wait_ge(s_w, 5 * DMA)
            with pe.Fori(1, NB - 1) as n:
                one_block(n, False, False)
            one_block(NB - 1, False, True)
            add_up(NB - 1, NU - 1)
            for j in range(HJ):
                mlp(NB - 1, j)

        @block.scalar
        def _(act):
            def high(n, g):
                gg = n * NG + g
                act.wait_ge(s_rows[g % RING], rows_by(n, g))
                if some(2 * gg - 3):
                    act.wait_ge(s_turned, 2 * gg - 3)
                src = rows[:, g % RING, :, :].rearrange("p t (f d) -> p (t f) d", d=D)
                for a in (0, 3):
                    last = act.activation(parts[:, g % 2, :, a, :], src, ACT.Copy)
                last.then_inc(s_hi, 1)

            def middle(n, g):
                act.wait_ge(s_rest, n * NG + g + 1)
                act.activation(parts[:, g % 2, :, 1, :],
                               rest[:, g % 2, :, :].rearrange("p t (f d) -> p (t f) d", d=D),
                               ACT.Copy).then_inc(s_mid, 1)

            def save_parts(n, g):
                act.wait_ge(s_turned, 2 * (n * NG + g) + 1)
                if some(n * NU - NU + LAST_USE_OF[g] + 1):
                    act.wait_ge(s_y, n * NU - NU + LAST_USE_OF[g] + 1)
                act.activation(xparts[:, GF * g:GF * (g + 1), :].rearrange("p f b -> p (f b)"),
                               turnb[:, :], ACT.Copy).then_inc(s_cols, 1)

            def save_rows(n, g):
                act.wait_ge(s_turned, 2 * (n * NG + g) + 2)
                if some(n * NU - NU + LAST_UNIT_OF[g] + 1):
                    act.wait_ge(s_prod, n * NU - NU + LAST_UNIT_OF[g] + 1)
                act.activation(xcols[:, g, :], turn[:, 0:BLK], ACT.Copy).then_inc(s_cols, 1)

            def save_z(n, tile):
                act.wait_ge(s_z, n * ZT + tile + 1)
                if tile < ZT - 1:
                    if some(n * HJ - HJ + H1T):
                        act.wait_ge(s_h, n * HJ - HJ + H1T)
                bank = H if tile == ZT - 1 else Z[tile % 2]
                act.activation(z[:, tile, :], bank[:, 0:BLK], ACT.Copy).then_inc(s_zs, 1)

            def save_h(n, j):
                act.wait_ge(s_h, n * HJ + j + 1)
                if j < H1T:
                    act.activation(h1[:, j, :], H[:, 0:BLK], ACT.Relu, bias=b1_sb[:, j:j + 1]).then_inc(s_hs, 1)
                elif j < H1T + H2T:
                    m = j - H1T
                    act.activation(h2[:, m, :], H[:, 0:BLK], ACT.Relu, bias=b2_sb[:, m:m + 1]).then_inc(s_hs, 1)
                else:
                    if some(n * DMA):
                        act.wait_ge(s_out, n * DMA)
                    act.activation(y[:, :], H[0:1, 0:BLK], ACT.Copy).then_inc(s_hs, 1)

            def tiles_done(u):
                return [t for t in range(ZT) if FIRST_CHUNK[u] < min(ZCH * (t + 1), CHUNKS) <= FIRST_CHUNK[u + 1]]

            def pieces(u):
                for p in pieces_at(u):
                    one, two, raw = piece(p)
                    act.wait_ge(s_min[p % 2], (p // 2 + 1) * GF * DMA)
                    act.activation(one, raw, ACT.Copy).then_inc(s_mh, 1)
                    act.wait_ge(s_mr, p + 1)
                    act.activation(two, raw, ACT.Copy).then_inc(s_mm, 1)

            def one_block(n, first, last):
                turns = turns_in(first, last)
                for u in range(NU):
                    if first:
                        pieces(u)
                    if u + PRE in turns:
                        g, ahead = turns[u + PRE]
                        high(n + ahead, g)
                        middle(n + ahead, g)
                    if u:
                        for t in tiles_done(u - 1):
                            save_z(n, t)
                    elif not first:
                        save_z(n - 1, ZT - 1)
                    if u in turns:
                        g, ahead = turns[u]
                        save_parts(n + ahead, g)
                    if u - 1 in turns:
                        g, ahead = turns[u - 1]
                        save_rows(n + ahead, g)
                    if u in MLP_AT and not first:
                        save_h(n - 1, MLP_AT.index(u))

            pieces(-1)
            for g in range(AHEAD):
                high(0, g)
                middle(0, g)
                save_parts(0, g)
                save_rows(0, g)
            one_block(0, True, False)
            act.wait_ge(s_w, 5 * DMA)
            with act.Fori(1, NB - 1) as n:
                one_block(n, False, False)
            one_block(NB - 1, False, True)
            save_z(NB - 1, ZT - 1)
            for j in range(HJ):
                save_h(NB - 1, j)

        @block.vector
        def _(dve):
            def left(n, g):
                dve.wait_ge(s_hi, n * NG + g + 1)
                dve.tensor_tensor(rest[:, g % 2, :, :].rearrange("p t (f d) -> p (t f) d", d=D),
                                  rows[:, g % RING, :, :].rearrange("p t (f d) -> p (t f) d", d=D),
                                  parts[:, g % 2, :, 0, :], ALU.subtract).then_inc(s_rest, 1)

            def low(n, g):
                dve.wait_ge(s_mid, n * NG + g + 1)
                dve.tensor_tensor(parts[:, g % 2, :, 2, :],
                                  rest[:, g % 2, :, :].rearrange("p t (f d) -> p (t f) d", d=D),
                                  parts[:, g % 2, :, 1, :], ALU.subtract).then_inc(s_parts, 1)

            def products(n, u):
                G, fields = UNITS[u]
                k = len(fields)
                dve.wait_ge(s_y, n * NU + u + 1)
                dve.wait_ge(s_cols, 2 * (n * NG + G) + 2)
                dve.tensor_tensor(prod[:, u % 2, 0:k, :], Y[u % 2][:, 0:k, :],
                                  xcols[:, G:G + 1, :].to_broadcast([P, k, BLK]), ALU.mult).then_inc(s_prod, 1)

            def pieces(u):
                for p in pieces_at(u):
                    one, two, raw = piece(p)
                    dve.wait_ge(s_mh, p + 1)
                    dve.tensor_tensor(raw, raw, one, ALU.subtract).then_inc(s_mr, 1)
                    dve.wait_ge(s_mm, p + 1)
                    dve.tensor_tensor(one[96:P], raw[96:P], two[96:P], ALU.subtract).then_inc(s_m, 1)

            def one_block(n, first, last):
                turns = turns_in(first, last)
                for u in range(NU):
                    if first:
                        pieces(u)
                    if u + PRE in turns:
                        g, ahead = turns[u + PRE]
                        left(n + ahead, g)
                    if u + PRE - 1 in turns:
                        g, ahead = turns[u + PRE - 1]
                        low(n + ahead, g)
                    products(n, u)

            pieces(-1)
            for g in range(AHEAD):
                left(0, g)
                low(0, g)
            one_block(0, True, False)
            with dve.Fori(1, NB - 1) as n:
                one_block(n, False, False)
            one_block(NB - 1, False, True)


def kernel(**inputs):
    import numpy as np
    import concourse.bacc as bacc
    from concourse.bass_utils import run_bass_kernel_spmd

    def pair(i, j):
        return i * (2 * FIELDS - i - 1) // 2 + j - i - 1

    bil = np.asarray(inputs["L0_rec_bilinear_matrices"])
    m_rows = np.zeros((D, CHUNKS, GF, D), bil.dtype)
    top1 = np.asarray(inputs["W_top1"])
    w1 = np.zeros((ZT * P, HID1), top1.dtype)
    c = 0
    for G, fields in UNITS:
        for i in fields:
            tile, q, o, _, _ = place(c)
            for s in range(GF):
                j = GF * G + s
                if j > i:
                    m_rows[:, c, s, :] = bil[pair(i, j)]
                    w1[tile * P + 32 * q + GF * o + s] = top1[pair(i, j)]
            c += 1
    pairs = FIELDS * (FIELDS - 1) // 2
    w1[ZT * P - DENSE:] = top1[pairs:]

    nc = bacc.Bacc("TRN2", target_bir_lowering=False, num_devices=1)
    arrays = {}

    def give(name, a):
        a = np.ascontiguousarray(a)
        arrays[name] = a
        return nc.dram_tensor(name, a.shape, mybir.dt.from_np(a.dtype), kind="ExternalInput").ap()

    args = [
        give("ids", inputs["ids"]), give("dense_ctx", inputs["dense_ctx"]),
        [give(f"tbl_{f}", inputs[f"tbl_{f}"]) for f in range(FIELDS)],
        give("m_rows", m_rows.reshape(D, CHUNKS * GF * D)), give("w1", w1),
        give("b1", np.asarray(inputs["b_top1"]).reshape(H1T, P).T), give("w2", inputs["W_top2"]),
        give("b2", np.asarray(inputs["b_top2"]).reshape(H2T, P).T),
        give("w3", np.asarray(inputs["W_top3"]).reshape(H2T, P).T),
        nc.dram_tensor("out_0", (BATCH, 1), F32, kind="ExternalOutput").ap(),
    ]
    tower(nc, *args)
    r = run_bass_kernel_spmd(nc, [arrays], core_ids=[0])
    return r.results[0]["out_0"]
```

```python
from contextlib import ExitStack

import concourse.bass as bass
from concourse import mybir

F32, BF16, I32 = mybir.dt.float32, mybir.dt.bfloat16, mybir.dt.int32
ALU, ACT = mybir.AluOpType, mybir.ActivationFunctionType

P = 128
BATCH, FIELDS, D, DENSE = 2048, 40, 32, 16
HID1, HID2 = 512, 256
BLK = 256
NB = BATCH // BLK
BT = BLK // P
GF = P // D
NG = FIELDS // GF
DMA = 16


def plan():
    units = []
    for G in range(NG):
        for a in range(G):
            units.append((G, a, [[(0, GF, GF * a + k)] for k in range(GF)]))
        i = GF * G
        one = [(0, 1, i + 3), (1, 2, i), (2, 3, i), (3, 4, i + 1)]
        two = [(0, 2, None), (2, 3, i + 1), (3, 4, i + 2)]
        units.append((G, G, [one, two]))
    if len(units) % 2:
        units[0:1] = [(0, 0, [c]) for c in units[0][2]]
    return units


UNITS = plan()
NU = len(UNITS)
FIRST_CHUNK = [sum(len(c) for _, _, c in UNITS[:u]) for u in range(NU + 1)]
CHUNKS = FIRST_CHUNK[NU]
LAST_UNIT_OF = [max(u for u in range(NU) if UNITS[u][0] == G) for G in range(NG)]
FIRST_UNIT_OF = [min(u for u in range(NU) if UNITS[u][0] == G) for G in range(NG)]
LAST_USE_OF = [max(u for u in range(NU) if UNITS[u][1] == g) for g in range(NG)]

SPAN = 8
ZCH = 4 * SPAN
ZT = -(-CHUNKS // ZCH)
H1T, H2T = HID1 // P, HID2 // P
HJ = H1T + H2T + 1

QUARTERS = P // D
PIECES = [8] + [32] * ((CHUNKS - 8) // 32)
PIECE_AT = [sum(PIECES[:p]) for p in range(len(PIECES) + 1)]
NP = len(PIECES)
WIDE = max(PIECES) // QUARTERS * P
assert PIECE_AT[NP] == CHUNKS and not any(n % QUARTERS for n in PIECES)
RING = 5
LAPS = NG // RING

AHEAD = 4
PRE = 3
TURN_AT = {g: FIRST_UNIT_OF[NG - 1] + 1 + 2 * g for g in range(AHEAD)}
TURN_AT |= {4: 3, 5: 7, 6: 12, 7: 18, 8: 25, 9: 33}
LATE = 6
TURN_FIRST = {g: FIRST_UNIT_OF[g] - (1 if g < LATE else 3) for g in range(1, NG)}
MLP_AT = [2, 3, 4, 5, 6, 7, 8]


def place(c):
    tile, r = divmod(c, ZCH)
    q, o = r % 4, r // 4
    return tile, q, o, o == 0, (o == SPAN - 1 or c + 4 >= CHUNKS)


class Turns:

    def __init__(self, first, last):
        self.high, self.low, self.parts, self.rows = {}, {}, {}, {}
        at = [(g, 0, TURN_FIRST[g]) for g in TURN_FIRST] if first else [(g, 0, TURN_AT[g]) for g in range(AHEAD, NG)]
        if not last:
            at += [(g, 1, TURN_AT[g]) for g in range(AHEAD)]
        for g, ahead, u in at:
            late = first and not ahead and g < LATE
            self.high[u if late else u - PRE] = (g, ahead)
            self.low[u if late else u - PRE + 1] = (g, ahead)
            self.parts[u] = (g, ahead)
            self.rows[u if late else u + 1] = (g, ahead)


def tower(nc, ids, dense, tables, m_wide, w1, b1, w2, b2, w3, out):
    ctx = ExitStack()
    with ctx:
        def sb(name, shape, dt):
            return ctx.enter_context(nc.sbuf_tensor(name, shape, dt))

        def sem(name):
            return ctx.enter_context(nc.semaphore(name))

        ident = sb("ident", [P, P], F32)
        identb = sb("identb", [P, P], BF16)
        sel = sb("sel", [P, GF * (SPAN - 1) + 32], F32)
        pass1 = sb("pass1", [P, CHUNKS, P], BF16)
        pass2 = sb("pass2", [P, CHUNKS, P], BF16)
        m_in = sb("m_in", [P, 2, WIDE], F32)
        m_parts = sb("m_parts", [P, 2, 3, WIDE], BF16)
        m_split = nc.dram_tensor("m_split", (NP, P, 3, WIDE), BF16, kind="Internal").ap()
        w1_sb = sb("w1_sb", [P, ZT, HID1], F32)
        w2_sb = sb("w2_sb", [P, H1T, HID2], F32)
        w3_sb = sb("w3_sb", [P, H2T], F32)
        b1_sb = sb("b1_sb", [P, H1T], F32)
        b2_sb = sb("b2_sb", [P, H2T], F32)
        idx_first = sb("idx_first", [P, BT, FIELDS], I32)
        idx = sb("idx", [P, LAPS, BT, FIELDS // LAPS], I32)
        rows = sb("rows", [P, RING, BT, P], F32)
        rest = sb("rest", [P, 2, BT, P], F32)
        parts = sb("parts", [P, 2, BT * GF, 4, D], BF16)
        xparts = sb("xparts", [P, FIELDS, BLK], BF16)
        xcols = sb("xcols", [P, NG, BLK], F32)
        prod = sb("prod", [P, 2, GF, BLK], F32)
        dpad = sb("dpad", [P, BT, 32], F32)
        z = sb("z", [P, ZT, BLK], F32)
        h1 = sb("h1", [P, H1T, BLK], F32)
        h2 = sb("h2", [P, H2T, BLK], F32)
        y = sb("y", [1, BLK], F32)
        Y = [ctx.enter_context(nc.psum_tensor(f"Y{k}", [P, GF, BLK], F32)) for k in range(2)]
        Z = [ctx.enter_context(nc.psum_tensor(f"Z{k}", [P, 512], F32)) for k in range(2)]
        turn = ctx.enter_context(nc.psum_tensor("turn", [P, 512], F32))
        H = ctx.enter_context(nc.psum_tensor("H", [P, 512], F32))
        turnb = turn[:, :].bitcast(BF16)

        s_zero = sem("s_zero")
        s_const = sem("s_const")
        s_idx_first = sem("s_idx_first")
        s_idx = [sem(f"s_idx{k}") for k in range(LAPS)]
        s_begun = sem("s_begun")
        s_rows = [sem(f"s_rows{k}") for k in range(RING)]
        s_hi = sem("s_hi")
        s_rest = sem("s_rest")
        s_mid = sem("s_mid")
        s_parts = sem("s_parts")
        s_turned = sem("s_turned")
        s_cols = sem("s_cols")
        s_y = sem("s_y")
        s_prod = sem("s_prod")
        s_z = sem("s_z")
        s_zs = sem("s_zs")
        s_h = sem("s_h")
        s_hs = sem("s_hs")
        s_min = [sem(f"s_min{k}") for k in range(2)]
        s_mh = sem("s_mh")
        s_mr = sem("s_mr")
        s_mm = sem("s_mm")
        s_ml = sem("s_ml")
        s_ms = [sem(f"s_ms{k}") for k in range(2)]
        s_m = [sem(f"s_m{p}") for p in range(NP)]
        s_w = sem("s_w")
        s_dense = sem("s_dense")
        s_out = sem("s_out")

        block = ctx.enter_context(nc.Block())

        def some(value):
            return not isinstance(value, int) or value > 0

        def rows_by(n, g):
            return (n * LAPS + g // RING + 1) * GF * BT * DMA

        def pieces_at(u):
            return [u + 2] if 0 <= u + 2 < NP else []

        @block.sync
        def _(sp):
            def load_idx(n, lap):
                if not isinstance(n, int):
                    for k in range(RING):
                        sp.wait_ge(s_rows[k], rows_by(n - 1, lap * RING + k))
                w = FIELDS // LAPS
                src = ids.rearrange("(n t p) f -> p n t f", t=BT, p=P)
                if isinstance(n, int):
                    src = src[:, n, :, lap * w:(lap + 1) * w]
                else:
                    src = src[:, bass.ds(n, 1), :, lap * w:(lap + 1) * w].rearrange("p n t f -> p (n t) f")
                sp.dma_start(idx[:, lap, :, :], src).then_inc(s_idx[lap], DMA)

            def load_dense(n):
                if some(n * ZT):
                    sp.wait_ge(s_z, n * ZT)
                src = dense.rearrange("(n t p) f -> p n t f", t=BT, p=P)
                if isinstance(n, int):
                    src = src[:, n, :, :]
                else:
                    src = src[:, bass.ds(n, 1), :, :].rearrange("p n t f -> p (n t) f")
                sp.dma_start(dpad[:, :, 32 - DENSE:32], src).then_inc(s_dense, DMA)

            def store(n):
                sp.wait_ge(s_hs, (n + 1) * HJ)
                dst = out.rearrange("(n b) o -> n (b o)", b=BLK)
                if isinstance(n, int):
                    dst = dst[n:n + 1, :]
                else:
                    dst = dst[bass.ds(n, 1), :]
                sp.dma_start(dst, y[:, :]).then_inc(s_out, DMA)

            sp.dma_start(idx_first[:, :, :], ids[0:BLK, :].rearrange("(t p) f -> p t f", p=P)).then_inc(s_idx_first, DMA)
            for lap in range(LAPS):
                load_idx(1, lap)
            sp.wait_ge(s_const, 1)
            def load_piece(p):
                w = PIECES[p] // QUARTERS * P
                at = PIECE_AT[p] // QUARTERS * P
                sp.dma_start(m_in[:, p % 2, 0:w], m_wide[:, at:at + w]).then_inc(s_min[p % 2], DMA)

            load_piece(0)
            load_piece(1)
            load_dense(0)
            for p in range(NP):
                w = PIECES[p] // QUARTERS * P
                sp.wait_ge(s_ml, p + 1)
                sp.dma_start(m_split[p, :, :, 0:w], m_parts[:, p % 2, :, 0:w]).then_inc(s_ms[p % 2], DMA)
                if p + 2 < NP:
                    load_piece(p + 2)
                sp.wait_ge(s_ms[p % 2], (p // 2 + 1) * DMA)
                for weights, row, part in ((pass1, 0, 0), (pass2, 0, 1), (pass1, 1, 0), (pass2, 1, 1),
                                           (pass1, 2, 0), (pass2, 2, 1), (pass1, 3, 2)):
                    dst = weights[D * row:D * (row + 1), PIECE_AT[p]:PIECE_AT[p + 1], :]
                    sp.dma_start(dst.rearrange("d (q c) n -> d q (c n)", q=QUARTERS),
                                 m_split[p, :, part, 0:w].rearrange("(q d) n -> d q n", d=D)).then_inc(s_m[p], DMA)
                if p == 3:
                    sp.dma_start(w1_sb[:, :, :], w1.rearrange("(t p) n -> p t n", p=P)).then_inc(s_w, DMA)
                    sp.dma_start(w2_sb[:, :, :], w2.rearrange("(t p) n -> p t n", p=P)).then_inc(s_w, DMA)
                    sp.dma_start(w3_sb[:, :], w3).then_inc(s_w, DMA)
                    sp.dma_start(b1_sb[:, :], b1).then_inc(s_w, DMA)
                    sp.dma_start(b2_sb[:, :], b2).then_inc(s_w, DMA)
            load_dense(1)
            with sp.Fori(0, NB - 2) as n:
                load_idx(n + 2, 0)
                store(n)
                load_idx(n + 2, 1)
                load_dense(n + 2)
            store(NB - 2)
            store(NB - 1)
            sp.wait_ge(s_out, NB * DMA)

        @block.gpsimd
        def _(pool):
            pool.memset(ident[:, :], 0.0).then_inc(s_zero, 1)
            pool.memset(identb[:, :], 0.0).then_inc(s_zero, 1)
            pool.memset(sel[:, :], 0.0).then_inc(s_zero, 1)
            pool.memset(dpad[:, :, 0:32 - DENSE], 0.0).then_inc(s_zero, 1)
            pool.wait_ge(s_zero, 4)
            for m in (ident, identb):
                pool.affine_select(out=m[:, :], in_=m[:, :], compare_op=ALU.not_equal, fill=1.0, base=0,
                                   pattern=[[-1, P]], channel_multiplier=1).then_inc(s_zero, 1)
            for s in range(GF):
                c = GF * (SPAN - 1) + s
                pool.wait_ge(s_zero, 6 + s)
                pool.memset(sel[D * s:D * (s + 1), c:c + 1], 1.0).then_inc(s_zero, 1)
            pool.wait_ge(s_zero, 6 + GF)
            pool.engine_nop().then_inc(s_const, 1)

            def gather(n):
                for lap in range(LAPS):
                    if isinstance(n, int):
                        pool.wait_ge(s_idx_first, DMA)
                    else:
                        pool.wait_ge(s_idx[lap], n * DMA)
                    for k in range(RING):
                        g = lap * RING + k
                        if some(2 * (n * NG + g - RING + 1)):
                            pool.wait_ge(s_turned, 2 * (n * NG + g - RING + 1))
                        pool.sem_inc(s_begun, 1)
                        for f in range(GF):
                            for t in range(BT):
                                at = GF * g + f if isinstance(n, int) else GF * k + f
                                which = idx_first[:, t, at:at + 1] if isinstance(n, int) else idx[:, lap, t, at:at + 1]
                                pool.indirect_dma_start(
                                    out=rows[:, k, t, D * f:D * (f + 1)], out_offset=None,
                                    in_=tables[GF * g + f],
                                    in_offset=bass.IndirectOffsetOnAxis(ap=which, axis=0),
                                ).then_inc(s_rows[k], DMA)

            gather(0)
            with pool.Fori(1, NB) as n:
                gather(n)

        @block.tensor
        def _(pe):
            def multiply(n, u, first):
                G, a, chunks = UNITS[u]
                if some(n * NU + u - 1):
                    pe.wait_ge(s_prod, n * NU + u - 1)
                pe.wait_ge(s_cols, 2 * (n * NG + a) + 1)
                for k, chunk in enumerate(chunks):
                    c = FIRST_CHUNK[u] + k
                    if first and c in PIECE_AT:
                        p = PIECE_AT.index(c)
                        pe.wait_ge(s_m[p], 7 * DMA)
                    for s0, s1, i in chunk:
                        x = xparts[:, GF * a if i is None else i, :]
                        last = pe.matmul(Y[u % 2][D * s0:D * s1, k, :], pass1[:, c, D * s0:D * s1], x,
                                         start=True, stop=i is None)
                    for s0, s1, i in chunk:
                        if i is not None:
                            last = pe.matmul(Y[u % 2][D * s0:D * s1, k, :], pass2[0:96, c, D * s0:D * s1],
                                             xparts[0:96, i, :], start=False, stop=True)
                last.then_inc(s_y, 1)

            def add_up(n, u):
                pe.wait_ge(s_prod, n * NU + u + 1)
                for k in range(len(UNITS[u][2])):
                    c = FIRST_CHUNK[u] + k
                    tile, q, o, start, stop = place(c)
                    final = tile == ZT - 1
                    bank = H if final else Z[tile % 2]
                    if c == ZCH * tile:
                        if final:
                            if some(n * HJ):
                                pe.wait_ge(s_hs, n * HJ)
                        elif tile < 2:
                            if some(n * ZT - ZT + tile + 5):
                                pe.wait_ge(s_zs, n * ZT - ZT + tile + 5)
                        else:
                            pe.wait_ge(s_zs, n * ZT + tile - 1)
                    last = pe.matmul(bank[32 * q:32 * q + 32, 0:BLK],
                                     sel[:, GF * (SPAN - 1 - o):GF * (SPAN - 1 - o) + 32],
                                     prod[:, u % 2, k, :], start=start, stop=stop)
                    if c % ZCH == ZCH - 1 or c == CHUNKS - 1:
                        last.then_inc(s_z, 1)
                    if final and q == 3 and start:
                        pe.wait_ge(s_dense, (n + 1) * DMA)
                        for t in range(BT):
                            pe.matmul(H[96:P, t * P:(t + 1) * P], dpad[:, t, :], ident[:, :],
                                      start=False, stop=False, skip_group_check=True)

            def turn_parts(n, g):
                gg = n * NG + g
                if some(2 * gg):
                    pe.wait_ge(s_cols, 2 * gg)
                pe.wait_ge(s_parts, gg + 1)
                for f in range(GF):
                    for t in range(BT):
                        last = pe.transpose(turnb[:, f * BLK + t * P:f * BLK + (t + 1) * P],
                                            parts[:, g % 2, t * GF + f, :, :].rearrange("p a d -> p (a d)"),
                                            identb[:, :])
                last.then_inc(s_turned, 1)

            def turn_rows(n, g):
                pe.wait_ge(s_cols, 2 * (n * NG + g) + 1)
                for t in range(BT):
                    last = pe.transpose(turn[:, t * P:(t + 1) * P], rows[:, g % RING, t, :], ident[:, :])
                last.then_inc(s_turned, 1)

            def mlp(n, j):
                if j == 0:
                    pe.wait_ge(s_zs, (n + 1) * ZT)
                else:
                    pe.wait_ge(s_hs, n * HJ + j)
                if j < H1T:
                    steps = [(w1_sb[:, k, j * P:(j + 1) * P], z[:, k, :]) for k in range(ZT)]
                elif j < H1T + H2T:
                    m = j - H1T
                    steps = [(w2_sb[:, k, m * P:(m + 1) * P], h1[:, k, :]) for k in range(H1T)]
                else:
                    steps = [(w3_sb[:, k:k + 1], h2[:, k, :]) for k in range(H2T)]
                for k, (w, x) in enumerate(steps):
                    last = pe.matmul(H[0:w.shape[1], 0:BLK], w, x, start=k == 0, stop=k == len(steps) - 1)
                last.then_inc(s_h, 1)

            def one_block(n, first, last):
                turns = Turns(first, last)
                for u in range(NU):
                    multiply(n, u, first)
                    if u:
                        add_up(n, u - 1)
                    elif not first:
                        add_up(n - 1, NU - 1)
                    if u in turns.parts:
                        g, ahead = turns.parts[u]
                        turn_parts(n + ahead, g)
                    if u in turns.rows:
                        g, ahead = turns.rows[u]
                        turn_rows(n + ahead, g)
                    if u in MLP_AT and not first:
                        mlp(n - 1, MLP_AT.index(u))

            pe.wait_ge(s_const, 1)
            turn_parts(0, 0)
            turn_rows(0, 0)
            one_block(0, True, False)
            pe.wait_ge(s_w, 5 * DMA)
            with pe.Fori(1, NB - 1) as n:
                one_block(n, False, False)
            one_block(NB - 1, False, True)
            add_up(NB - 1, NU - 1)
            for j in range(HJ):
                mlp(NB - 1, j)

        @block.scalar
        def _(act):
            def high(n, g):
                gg = n * NG + g
                act.wait_ge(s_rows[g % RING], rows_by(n, g))
                if some(2 * gg - 3):
                    act.wait_ge(s_turned, 2 * gg - 3)
                src = rows[:, g % RING, :, :].rearrange("p t (f d) -> p (t f) d", d=D)
                for a in (0, 3):
                    last = act.activation(parts[:, g % 2, :, a, :], src, ACT.Copy)
                last.then_inc(s_hi, 1)

            def middle(n, g):
                act.wait_ge(s_rest, n * NG + g + 1)
                act.activation(parts[:, g % 2, :, 1, :],
                               rest[:, g % 2, :, :].rearrange("p t (f d) -> p (t f) d", d=D),
                               ACT.Copy).then_inc(s_mid, 1)

            def save_parts(n, g):
                act.wait_ge(s_turned, 2 * (n * NG + g) + 1)
                if some(n * NU - NU + LAST_USE_OF[g] + 1):
                    act.wait_ge(s_y, n * NU - NU + LAST_USE_OF[g] + 1)
                act.activation(xparts[:, GF * g:GF * (g + 1), :].rearrange("p f b -> p (f b)"),
                               turnb[:, :], ACT.Copy).then_inc(s_cols, 1)

            def save_rows(n, g):
                act.wait_ge(s_turned, 2 * (n * NG + g) + 2)
                if some(n * NU - NU + LAST_UNIT_OF[g] + 1):
                    act.wait_ge(s_prod, n * NU - NU + LAST_UNIT_OF[g] + 1)
                act.activation(xcols[:, g, :], turn[:, 0:BLK], ACT.Copy).then_inc(s_cols, 1)

            def save_z(n, tile):
                act.wait_ge(s_z, n * ZT + tile + 1)
                if tile < ZT - 1:
                    if some(n * HJ - HJ + H1T):
                        act.wait_ge(s_h, n * HJ - HJ + H1T)
                bank = H if tile == ZT - 1 else Z[tile % 2]
                act.activation(z[:, tile, :], bank[:, 0:BLK], ACT.Copy).then_inc(s_zs, 1)

            def save_h(n, j):
                act.wait_ge(s_h, n * HJ + j + 1)
                if j < H1T:
                    act.activation(h1[:, j, :], H[:, 0:BLK], ACT.Relu, bias=b1_sb[:, j:j + 1]).then_inc(s_hs, 1)
                elif j < H1T + H2T:
                    m = j - H1T
                    act.activation(h2[:, m, :], H[:, 0:BLK], ACT.Relu, bias=b2_sb[:, m:m + 1]).then_inc(s_hs, 1)
                else:
                    if some(n * DMA):
                        act.wait_ge(s_out, n * DMA)
                    act.activation(y[:, :], H[0:1, 0:BLK], ACT.Copy).then_inc(s_hs, 1)

            def tiles_done(u):
                return [t for t in range(ZT) if FIRST_CHUNK[u] < min(ZCH * (t + 1), CHUNKS) <= FIRST_CHUNK[u + 1]]

            def pieces(u):
                for p in pieces_at(u):
                    w = PIECES[p] // QUARTERS * P
                    act.wait_ge(s_min[p % 2], (p // 2 + 1) * DMA)
                    if p >= 2:
                        act.wait_ge(s_ms[p % 2], p // 2 * DMA)
                    act.activation(m_parts[:, p % 2, 0, 0:w], m_in[:, p % 2, 0:w], ACT.Copy).then_inc(s_mh, 1)
                    act.wait_ge(s_mr, p + 1)
                    act.activation(m_parts[:, p % 2, 1, 0:w], m_in[:, p % 2, 0:w], ACT.Copy).then_inc(s_mm, 1)

            def one_block(n, first, last):
                turns = Turns(first, last)
                for u in range(NU):
                    if first:
                        pieces(u)
                    if u in turns.high:
                        g, ahead = turns.high[u]
                        high(n + ahead, g)
                        middle(n + ahead, g)
                    if u:
                        for t in tiles_done(u - 1):
                            save_z(n, t)
                    elif not first:
                        save_z(n - 1, ZT - 1)
                    if u in turns.parts:
                        g, ahead = turns.parts[u]
                        save_parts(n + ahead, g)
                    if u in turns.rows:
                        g, ahead = turns.rows[u]
                        save_rows(n + ahead, g)
                    if u in MLP_AT and not first:
                        save_h(n - 1, MLP_AT.index(u))

            pieces(-2)
            pieces(-1)
            high(0, 0)
            middle(0, 0)
            save_parts(0, 0)
            save_rows(0, 0)
            one_block(0, True, False)
            act.wait_ge(s_w, 5 * DMA)
            with act.Fori(1, NB - 1) as n:
                one_block(n, False, False)
            one_block(NB - 1, False, True)
            save_z(NB - 1, ZT - 1)
            for j in range(HJ):
                save_h(NB - 1, j)

        @block.vector
        def _(dve):
            def left(n, g):
                dve.wait_ge(s_hi, n * NG + g + 1)
                dve.tensor_tensor(rest[:, g % 2, :, :].rearrange("p t (f d) -> p (t f) d", d=D),
                                  rows[:, g % RING, :, :].rearrange("p t (f d) -> p (t f) d", d=D),
                                  parts[:, g % 2, :, 0, :], ALU.subtract).then_inc(s_rest, 1)

            def low(n, g):
                dve.wait_ge(s_mid, n * NG + g + 1)
                dve.tensor_tensor(parts[:, g % 2, :, 2, :],
                                  rest[:, g % 2, :, :].rearrange("p t (f d) -> p (t f) d", d=D),
                                  parts[:, g % 2, :, 1, :], ALU.subtract).then_inc(s_parts, 1)

            def products(n, u):
                G, _, chunks = UNITS[u]
                k = len(chunks)
                dve.wait_ge(s_y, n * NU + u + 1)
                dve.wait_ge(s_cols, 2 * (n * NG + G) + 2)
                dve.tensor_tensor(prod[:, u % 2, 0:k, :], Y[u % 2][:, 0:k, :],
                                  xcols[:, G:G + 1, :].to_broadcast([P, k, BLK]), ALU.mult).then_inc(s_prod, 1)

            def pieces(u):
                for p in pieces_at(u):
                    w = PIECES[p] // QUARTERS * P
                    raw = m_in[:, p % 2, 0:w]
                    dve.wait_ge(s_mh, p + 1)
                    dve.tensor_tensor(raw, raw, m_parts[:, p % 2, 0, 0:w], ALU.subtract).then_inc(s_mr, 1)
                    dve.wait_ge(s_mm, p + 1)
                    dve.tensor_tensor(m_parts[:, p % 2, 2, 0:w], raw, m_parts[:, p % 2, 1, 0:w],
                                      ALU.subtract).then_inc(s_ml, 1)

            def one_block(n, first, last):
                turns = Turns(first, last)
                for u in range(NU):
                    if first:
                        pieces(u)
                    products(n, u)
                    if u in turns.high:
                        g, ahead = turns.high[u]
                        left(n + ahead, g)
                    if u in turns.low:
                        g, ahead = turns.low[u]
                        low(n + ahead, g)

            pieces(-2)
            pieces(-1)
            left(0, 0)
            low(0, 0)
            one_block(0, True, False)
            with dve.Fori(1, NB - 1) as n:
                one_block(n, False, False)
            one_block(NB - 1, False, True)


def kernel(**inputs):
    import numpy as np
    import concourse.bacc as bacc
    from concourse.bass_utils import run_bass_kernel_spmd

    def pair(i, j):
        return i * (2 * FIELDS - i - 1) // 2 + j - i - 1

    bil = np.asarray(inputs["L0_rec_bilinear_matrices"])
    m_rows = np.zeros((D, CHUNKS, GF, D), bil.dtype)
    top1 = np.asarray(inputs["W_top1"])
    w1 = np.zeros((ZT * P, HID1), top1.dtype)
    for u, (G, _, chunks) in enumerate(UNITS):
        for k, chunk in enumerate(chunks):
            c = FIRST_CHUNK[u] + k
            tile, q, o, _, _ = place(c)
            for s0, s1, i in chunk:
                for s in range(s0, s1):
                    j = GF * G + s
                    if i is not None:
                        at = pair(min(i, j), max(i, j))
                        m_rows[:, c, s, :] = bil[at] if i < j else bil[at].T
                        w1[tile * P + 32 * q + GF * o + s] = top1[at]
    m_wide = np.concatenate([
        m_rows[:, a:b].reshape(D, QUARTERS, -1).transpose(1, 0, 2).reshape(P, -1)
        for a, b in zip(PIECE_AT, PIECE_AT[1:])], axis=1)
    pairs = FIELDS * (FIELDS - 1) // 2
    w1[ZT * P - DENSE:] = top1[pairs:]

    nc = bacc.Bacc("TRN2", target_bir_lowering=False, num_devices=1)
    arrays = {}

    def give(name, a):
        a = np.ascontiguousarray(a)
        arrays[name] = a
        return nc.dram_tensor(name, a.shape, mybir.dt.from_np(a.dtype), kind="ExternalInput").ap()

    args = [
        give("ids", inputs["ids"]), give("dense_ctx", inputs["dense_ctx"]),
        [give(f"tbl_{f}", inputs[f"tbl_{f}"]) for f in range(FIELDS)],
        give("m_wide", m_wide), give("w1", w1),
        give("b1", np.asarray(inputs["b_top1"]).reshape(H1T, P).T), give("w2", inputs["W_top2"]),
        give("b2", np.asarray(inputs["b_top2"]).reshape(H2T, P).T),
        give("w3", np.asarray(inputs["W_top3"]).reshape(H2T, P).T),
        nc.dram_tensor("out_0", (BATCH, 1), F32, kind="ExternalOutput").ap(),
    ]
    tower(nc, *args)
    r = run_bass_kernel_spmd(nc, [arrays], core_ids=[0])
    return r.results[0]["out_0"]
```

```python
from contextlib import ExitStack

import concourse.bass as bass
from concourse import mybir

F32, BF16, I32 = mybir.dt.float32, mybir.dt.bfloat16, mybir.dt.int32
ALU, ACT = mybir.AluOpType, mybir.ActivationFunctionType

P = 128
BATCH, FIELDS, D, DENSE = 2048, 40, 32, 16
HID1, HID2 = 512, 256
BLK = 256
NB = BATCH // BLK
BT = BLK // P
GF = P // D
NG = FIELDS // GF
DMA = 16


def plan():
    units = []
    for G in range(NG):
        for a in range(G):
            units.append((G, a, [[(0, GF, GF * a + k)] for k in range(GF)]))
        i = GF * G
        one = [(0, 1, i + 3), (1, 2, i), (2, 3, i), (3, 4, i + 1)]
        two = [(0, 2, None), (2, 3, i + 1), (3, 4, i + 2)]
        units.append((G, G, [one, two]))
    if len(units) % 2:
        units[0:1] = [(0, 0, [c]) for c in units[0][2]]
    return units


UNITS = plan()
NU = len(UNITS)
FIRST_CHUNK = [sum(len(c) for _, _, c in UNITS[:u]) for u in range(NU + 1)]
CHUNKS = FIRST_CHUNK[NU]
LAST_UNIT_OF = [max(u for u in range(NU) if UNITS[u][0] == G) for G in range(NG)]
FIRST_UNIT_OF = [min(u for u in range(NU) if UNITS[u][0] == G) for G in range(NG)]
LAST_USE_OF = [max(u for u in range(NU) if UNITS[u][1] == g) for g in range(NG)]

SPAN = 8
ZCH = 4 * SPAN
ZT = -(-CHUNKS // ZCH)
H1T, H2T = HID1 // P, HID2 // P
HJ = H1T + H2T + 1

QUARTERS = P // D
PIECES = [8] + [32] * ((CHUNKS - 8) // 32)
PIECE_AT = [sum(PIECES[:p]) for p in range(len(PIECES) + 1)]
NP = len(PIECES)
WIDE = max(PIECES) // QUARTERS * P
assert PIECE_AT[NP] == CHUNKS and not any(n % QUARTERS for n in PIECES)
SPLIT_AT = {2: 2, 3: 6, 4: 12, 5: 19, 6: 27}
RING = 5
LAPS = NG // RING

LAG = 2
PRODS = 4
AHEAD = 5
TURN_AT = {0: 43, 1: 46, 2: 48, 3: 50, 4: 52, 5: 1, 6: 6, 7: 11, 8: 18, 9: 26}
PROMPT = 6
TURN_FIRST = {g: FIRST_UNIT_OF[g] - a for g, a in enumerate((2, 2, 2, 2, 3, 3, 4, 5, 7), 1)}
MLP_AT = [3, 4, 5, 6, 7, 8, 9]
STORE_AT = 10
assert NU % PRODS == 0


def place(c):
    tile, r = divmod(c, ZCH)
    q, o = r % 4, r // 4
    return tile, q, o, o == 0, (o == SPAN - 1 or c + 4 >= CHUNKS)


def turns_in(first, last):
    at = {u: (g, 0) for g, u in TURN_FIRST.items()} if first else {TURN_AT[g]: (g, 0) for g in range(AHEAD, NG)}
    if not last:
        at |= {TURN_AT[g]: (g, 1) for g in range(AHEAD)}
    return at


def lefts_in(first, last):
    return {u + (0 if first and not ahead else 1): (g, ahead) for u, (g, ahead) in turns_in(first, last).items()}


def lows_in(first, last):
    return {u + (2 if ahead or not first else 0 if g < PROMPT else 1): (g, ahead)
            for u, (g, ahead) in turns_in(first, last).items()}


def tower(nc, ids, dense, tables, m_wide, w1, b1, w2, b2, w3, out):
    ctx = ExitStack()
    with ctx:
        def sb(name, shape, dt):
            return ctx.enter_context(nc.sbuf_tensor(name, shape, dt))

        def sem(name):
            return ctx.enter_context(nc.semaphore(name))

        ident = sb("ident", [P, P], F32)
        sel = sb("sel", [P, GF * (SPAN - 1) + 32], F32)
        pass1 = sb("pass1", [P, CHUNKS, P], BF16)
        pass2 = sb("pass2", [P, CHUNKS, P], BF16)
        m_in = sb("m_in", [P, 2, WIDE], F32)
        shared = sb("shared", [P, 3 * WIDE], F32)
        m_parts = shared[:, :].bitcast(BF16).rearrange("p (k a n) -> p k a n", k=2, a=3)
        m_split = nc.dram_tensor("m_split", (NP, P, 3, WIDE), BF16, kind="Internal").ap()
        w1_sb = sb("w1_sb", [P, ZT, HID1], F32)
        w2_sb = sb("w2_sb", [P, H1T, HID2], F32)
        w3_sb = sb("w3_sb", [P, H2T], F32)
        b1_sb = sb("b1_sb", [P, H1T], F32)
        b2_sb = sb("b2_sb", [P, H2T], F32)
        idx_first = sb("idx_first", [P, BT, FIELDS], I32)
        idx = sb("idx", [P, LAPS, BT, FIELDS // LAPS], I32)
        rows = sb("rows", [P, RING, BT, P], F32)
        rest = sb("rest", [P, 2, BLK], F32)
        parts = sb("parts", [P, 2, 3, BLK], BF16)
        x_split = nc.dram_tensor("x_split", (NG, P, 3, BLK), BF16, kind="Internal").ap()
        xparts = sb("xparts", [P, FIELDS, BLK], BF16)
        xcols = sb("xcols", [P, NG, BLK], F32)
        prod = sb("prod", [P, PRODS, GF, BLK], F32)
        dpad = sb("dpad", [P, BT, 32], F32)
        z = sb("z", [P, ZT, BLK], F32)
        h1 = shared[:, 0:H1T * BLK].rearrange("p (k b) -> p k b", k=H1T)
        h2 = shared[:, H1T * BLK:(H1T + H2T) * BLK].rearrange("p (k b) -> p k b", k=H2T)
        y = sb("y", [1, BLK], F32)
        Y = [ctx.enter_context(nc.psum_tensor(f"Y{k}", [P, GF, BLK], F32)) for k in range(2)]
        Z = [ctx.enter_context(nc.psum_tensor(f"Z{k}", [P, 512], F32)) for k in range(2)]
        turn = ctx.enter_context(nc.psum_tensor("turn", [P, 512], F32))
        H = ctx.enter_context(nc.psum_tensor("H", [P, 512], F32))

        s_zero = sem("s_zero")
        s_const = sem("s_const")
        s_idx_first = sem("s_idx_first")
        s_idx = [sem(f"s_idx{k}") for k in range(LAPS)]
        s_begun = sem("s_begun")
        s_rows = [sem(f"s_rows{k}") for k in range(RING)]
        s_turned = sem("s_turned")
        s_cols = sem("s_cols")
        s_hi = sem("s_hi")
        s_rest = sem("s_rest")
        s_mid = sem("s_mid")
        s_parts = sem("s_parts")
        s_xs = [sem(f"s_xs{k}") for k in range(2)]
        s_x = [sem(f"s_x{k}") for k in range(2)]
        s_y = sem("s_y")
        s_prod = sem("s_prod")
        s_z = sem("s_z")
        s_zs = sem("s_zs")
        s_h = sem("s_h")
        s_hs = sem("s_hs")
        s_min = [sem(f"s_min{k}") for k in range(2)]
        s_mh = sem("s_mh")
        s_mr = sem("s_mr")
        s_mm = sem("s_mm")
        s_ml = sem("s_ml")
        s_ms = [sem(f"s_ms{k}") for k in range(2)]
        s_m = [sem(f"s_m{p}") for p in range(NP)]
        s_w = sem("s_w")
        s_dense = sem("s_dense")
        s_out = sem("s_out")

        block = ctx.enter_context(nc.Block())

        def some(value):
            return not isinstance(value, int) or value > 0

        def rows_by(n, g):
            return (n * LAPS + g // RING + 1) * GF * BT * DMA

        def tail_bank(j):
            if j == 0:
                return turn[:, 0:BLK]
            if j <= 4:
                return Y[(j - 1) // 2][:, 2 * ((j - 1) % 2), :]
            return Z[j - 5][:, 0:BLK]

        @block.sync
        def _(sp):
            def load_idx(n, lap):
                if some(n - 1):
                    for k in range(RING):
                        sp.wait_ge(s_rows[k], rows_by(n - 1, lap * RING + k))
                w = FIELDS // LAPS
                src = ids.rearrange("(n t p) f -> p n t f", t=BT, p=P)
                if isinstance(n, int):
                    src = src[:, n, :, lap * w:(lap + 1) * w]
                else:
                    src = src[:, bass.ds(n, 1), :, lap * w:(lap + 1) * w].rearrange("p n t f -> p (n t) f")
                sp.dma_start(idx[:, lap, :, :], src).then_inc(s_idx[lap], DMA)

            def load_dense(n):
                if some(n * ZT):
                    sp.wait_ge(s_z, n * ZT)
                src = dense.rearrange("(n t p) f -> p n t f", t=BT, p=P)
                if isinstance(n, int):
                    src = src[:, n, :, :]
                else:
                    src = src[:, bass.ds(n, 1), :, :].rearrange("p n t f -> p (n t) f")
                sp.dma_start(dpad[:, :, 32 - DENSE:32], src).then_inc(s_dense, DMA)

            def spread(n, g):
                gg = n * NG + g
                sp.wait_ge(s_parts, gg + 1)
                lap = n * (NG // 2) + g // 2
                if some(lap):
                    sp.wait_ge(s_x[g % 2], lap * 4 * DMA)
                sp.dma_start(x_split[g, :, :, :], parts[:, g % 2, :, :]).then_inc(s_xs[g % 2], DMA)
                if some(n * NU - NU + LAST_USE_OF[g] + 1):
                    sp.wait_ge(s_y, n * NU - NU + LAST_USE_OF[g] + 1)
                sp.wait_ge(s_xs[g % 2], (lap + 1) * DMA)
                for row, part in enumerate((0, 1, 2, 0)):
                    sp.dma_start(xparts[D * row:D * (row + 1), GF * g:GF * (g + 1), :],
                                 x_split[g, :, part, :].rearrange("(f d) b -> d f b", d=D)).then_inc(s_x[g % 2], DMA)

            def store(n):
                sp.wait_ge(s_hs, (n + 1) * HJ)
                dst = out.rearrange("(n b) o -> n (b o)", b=BLK)
                if isinstance(n, int):
                    dst = dst[n:n + 1, :]
                else:
                    dst = dst[bass.ds(n, 1), :]
                sp.dma_start(dst, y[:, :]).then_inc(s_out, DMA)

            sp.dma_start(idx_first[:, :, :], ids[0:BLK, :].rearrange("(t p) f -> p t f", p=P)).then_inc(s_idx_first, DMA)
            for lap in range(LAPS):
                load_idx(1, lap)
            sp.wait_ge(s_const, 1)

            def load_mlp():
                sp.dma_start(w1_sb[:, :, :], w1.rearrange("(t p) n -> p t n", p=P)).then_inc(s_w, DMA)
                sp.dma_start(w2_sb[:, :, :], w2.rearrange("(t p) n -> p t n", p=P)).then_inc(s_w, DMA)
                sp.dma_start(w3_sb[:, :], w3).then_inc(s_w, DMA)
                sp.dma_start(b1_sb[:, :], b1).then_inc(s_w, DMA)
                sp.dma_start(b2_sb[:, :], b2).then_inc(s_w, DMA)

            def one_block(n, first, last):
                turns = turns_in(first, last)
                for u in range(NU):
                    if u in turns:
                        g, ahead = turns[u]
                        spread(n + ahead, g)
                        if g in (RING, NG - 1) and not first and not last:
                            load_idx(n + 1, g // RING if g == NG - 1 else 0)
                    if u == LAG + 1:
                        if first:
                            load_mlp()
                        else:
                            load_dense(n)
                    if u == STORE_AT and not first:
                        store(n - 1)

            load_dense(0)
            spread(0, 0)
            one_block(0, True, False)
            with sp.Fori(1, NB - 1) as n:
                one_block(n, False, False)
            one_block(NB - 1, False, True)
            store(NB - 1)
            sp.wait_ge(s_out, NB * DMA)

        @block.gpsimd
        def _(pool):
            pool.memset(ident[:, :], 0.0).then_inc(s_zero, 1)
            pool.memset(sel[:, :], 0.0).then_inc(s_zero, 1)
            pool.memset(dpad[:, :, 0:32 - DENSE], 0.0).then_inc(s_zero, 1)
            pool.wait_ge(s_zero, 3)
            pool.affine_select(out=ident[:, :], in_=ident[:, :], compare_op=ALU.not_equal, fill=1.0, base=0,
                               pattern=[[-1, P]], channel_multiplier=1).then_inc(s_zero, 1)
            for s in range(GF):
                c = GF * (SPAN - 1) + s
                pool.wait_ge(s_zero, 4 + s)
                pool.memset(sel[D * s:D * (s + 1), c:c + 1], 1.0).then_inc(s_zero, 1)
            pool.wait_ge(s_zero, 4 + GF)
            pool.engine_nop().then_inc(s_const, 1)

            def gather(n):
                for lap in range(LAPS):
                    if isinstance(n, int):
                        pool.wait_ge(s_idx_first, DMA)
                    else:
                        pool.wait_ge(s_idx[lap], n * DMA)
                    for k in range(RING):
                        g = lap * RING + k
                        if some(n * NG + g - RING + 1):
                            pool.wait_ge(s_turned, n * NG + g - RING + 1)
                        pool.sem_inc(s_begun, 1)
                        for f in range(GF):
                            for t in range(BT):
                                at = GF * g + f if isinstance(n, int) else GF * k + f
                                which = idx_first[:, t, at:at + 1] if isinstance(n, int) else idx[:, lap, t, at:at + 1]
                                pool.indirect_dma_start(
                                    out=rows[:, k, t, D * f:D * (f + 1)], out_offset=None,
                                    in_=tables[GF * g + f],
                                    in_offset=bass.IndirectOffsetOnAxis(ap=which, axis=0),
                                ).then_inc(s_rows[k], DMA)

            gather(0)
            with pool.Fori(1, NB) as n:
                gather(n)

        @block.tensor
        def _(pe):
            def multiply(n, u, first):
                G, a, chunks = UNITS[u]
                if some(n * NU + u - 1):
                    pe.wait_ge(s_prod, n * NU + u - 1)
                pe.wait_ge(s_x[a % 2], (n * (NG // 2) + a // 2 + 1) * 4 * DMA)
                for k, chunk in enumerate(chunks):
                    c = FIRST_CHUNK[u] + k
                    if first and c in PIECE_AT:
                        p = PIECE_AT.index(c)
                        pe.wait_ge(s_m[p], 7 * DMA)
                    for s0, s1, i in chunk:
                        x = xparts[:, GF * a if i is None else i, :]
                        last = pe.matmul(Y[u % 2][D * s0:D * s1, k, :], pass1[:, c, D * s0:D * s1], x,
                                         start=True, stop=i is None)
                    for s0, s1, i in chunk:
                        if i is not None:
                            last = pe.matmul(Y[u % 2][D * s0:D * s1, k, :], pass2[0:96, c, D * s0:D * s1],
                                             xparts[0:96, i, :], start=False, stop=True)
                last.then_inc(s_y, 1)

            def add_up(n, u):
                pe.wait_ge(s_prod, n * NU + u + 1)
                for k in range(len(UNITS[u][2])):
                    c = FIRST_CHUNK[u] + k
                    tile, q, o, start, stop = place(c)
                    final = tile == ZT - 1
                    bank = H if final else Z[tile % 2]
                    if c == ZCH * tile:
                        if final:
                            if some(n * HJ):
                                pe.wait_ge(s_hs, n * HJ)
                        elif tile < 2:
                            if some(n * ZT - ZT + tile + 5):
                                pe.wait_ge(s_zs, n * ZT - ZT + tile + 5)
                        else:
                            pe.wait_ge(s_zs, n * ZT + tile - 1)
                    last = pe.matmul(bank[32 * q:32 * q + 32, 0:BLK],
                                     sel[:, GF * (SPAN - 1 - o):GF * (SPAN - 1 - o) + 32],
                                     prod[:, u % PRODS, k, :], start=start, stop=stop)
                    if c % ZCH == ZCH - 1 or c == CHUNKS - 1:
                        last.then_inc(s_z, 1)
                    if final and q == 3 and start:
                        pe.wait_ge(s_dense, (n + 1) * DMA)
                        for t in range(BT):
                            pe.matmul(H[96:P, t * P:(t + 1) * P], dpad[:, t, :], ident[:, :],
                                      start=False, stop=False, skip_group_check=True)

            def turn_rows(n, g):
                if some(n * NG + g):
                    pe.wait_ge(s_cols, n * NG + g)
                pe.wait_ge(s_rows[g % RING], rows_by(n, g))
                for t in range(BT):
                    last = pe.transpose(turn[:, t * P:(t + 1) * P], rows[:, g % RING, t, :], ident[:, :])
                last.then_inc(s_turned, 1)

            def mlp(n, j):
                if j == 0:
                    pe.wait_ge(s_zs, (n + 1) * ZT)
                else:
                    pe.wait_ge(s_hs, n * HJ + j)
                if j < H1T:
                    steps = [(w1_sb[:, k, j * P:(j + 1) * P], z[:, k, :]) for k in range(ZT)]
                elif j < H1T + H2T:
                    m = j - H1T
                    steps = [(w2_sb[:, k, m * P:(m + 1) * P], h1[:, k, :]) for k in range(H1T)]
                else:
                    steps = [(w3_sb[:, k:k + 1], h2[:, k, :]) for k in range(H2T)]
                for k, (w, x) in enumerate(steps):
                    last = pe.matmul(H[0:w.shape[1], 0:BLK], w, x, start=k == 0, stop=k == len(steps) - 1)
                last.then_inc(s_h, 1)

            def hidden_1(j, tiles):
                pe.wait_ge(s_zs, (NB - 1) * ZT + tiles[-1] + 1)
                if j > 0:
                    pe.wait_ge(s_prod, NB * NU)
                for k in tiles:
                    last = pe.matmul(tail_bank(j)[:, :], w1_sb[:, k, j * P:(j + 1) * P], z[:, k, :],
                                     start=k == 0, stop=k == ZT - 1)
                if ZT - 1 in tiles:
                    last.then_inc(s_h, 1)

            def hidden_2_and_y():
                for m in range(H2T):
                    for k in range(H1T):
                        pe.wait_ge(s_hs, (NB - 1) * HJ + k + 1)
                        last = pe.matmul(tail_bank(H1T + m)[:, :], w2_sb[:, k, m * P:(m + 1) * P], h1[:, k, :],
                                         start=k == 0, stop=k == H1T - 1)
                    last.then_inc(s_h, 1)
                for k in range(H2T):
                    pe.wait_ge(s_hs, (NB - 1) * HJ + H1T + k + 1)
                    last = pe.matmul(tail_bank(HJ - 1)[0:1, :], w3_sb[:, k:k + 1], h2[:, k, :],
                                     start=k == 0, stop=k == H2T - 1)
                last.then_inc(s_h, 1)

            def one_block(n, first, last):
                turns = turns_in(first, last)
                for u in range(NU):
                    multiply(n, u, first)
                    if u >= LAG:
                        add_up(n, u - LAG)
                    elif not first:
                        add_up(n - 1, NU + u - LAG)
                    if u in turns:
                        g, ahead = turns[u]
                        turn_rows(n + ahead, g)
                    if u in MLP_AT and not first:
                        mlp(n - 1, MLP_AT.index(u))

            pe.wait_ge(s_const, 1)
            turn_rows(0, 0)
            one_block(0, True, False)
            pe.wait_ge(s_w, 5 * DMA)
            with pe.Fori(1, NB - 1) as n:
                one_block(n, False, False)
            one_block(NB - 1, False, True)
            add_up(NB - 1, NU - 2)
            hidden_1(0, range(ZT - 1))
            add_up(NB - 1, NU - 1)
            for j in range(1, H1T):
                hidden_1(j, range(ZT - 1))
            for j in range(H1T):
                hidden_1(j, range(ZT - 1, ZT))
            hidden_2_and_y()

        @block.scalar
        def _(act):
            def save_rows(n, g):
                act.wait_ge(s_turned, n * NG + g + 1)
                if some(n * NU - NU + LAST_UNIT_OF[g] + 1):
                    act.wait_ge(s_prod, n * NU - NU + LAST_UNIT_OF[g] + 1)
                act.activation(xcols[:, g, :], turn[:, 0:BLK], ACT.Copy).then_inc(s_cols, 1)

            def high(n, g):
                act.wait_ge(s_cols, n * NG + g + 1)
                lap = n * (NG // 2) + g // 2
                if some(lap):
                    act.wait_ge(s_xs[g % 2], lap * DMA)
                act.activation(parts[:, g % 2, 0, :], xcols[:, g, :], ACT.Copy).then_inc(s_hi, 1)

            def middle(n, g):
                act.wait_ge(s_rest, n * NG + g + 1)
                act.activation(parts[:, g % 2, 1, :], rest[:, g % 2, :], ACT.Copy).then_inc(s_mid, 1)

            def save_z(n, tile):
                act.wait_ge(s_z, n * ZT + tile + 1)
                if tile < ZT - 1:
                    if some(n * HJ - HJ + H1T):
                        act.wait_ge(s_h, n * HJ - HJ + H1T)
                bank = H if tile == ZT - 1 else Z[tile % 2]
                act.activation(z[:, tile, :], bank[:, 0:BLK], ACT.Copy).then_inc(s_zs, 1)

            def save_h(n, j, bank=H[:, 0:BLK]):
                act.wait_ge(s_h, n * HJ + j + 1)
                if j < H1T:
                    act.activation(h1[:, j, :], bank, ACT.Relu, bias=b1_sb[:, j:j + 1]).then_inc(s_hs, 1)
                elif j < H1T + H2T:
                    m = j - H1T
                    act.activation(h2[:, m, :], bank, ACT.Relu, bias=b2_sb[:, m:m + 1]).then_inc(s_hs, 1)
                else:
                    if some(n * DMA):
                        act.wait_ge(s_out, n * DMA)
                    act.activation(y[:, :], bank[0:1, :], ACT.Copy).then_inc(s_hs, 1)

            def tiles_done(u):
                return [t for t in range(ZT) if FIRST_CHUNK[u] < min(ZCH * (t + 1), CHUNKS) <= FIRST_CHUNK[u + 1]]

            def load_piece(p):
                w = PIECES[p] // QUARTERS * P
                at = PIECE_AT[p] // QUARTERS * P
                if p >= 2:
                    act.wait_ge(s_ml, p - 1)
                act.dma_start(m_in[:, p % 2, 0:w], m_wide[:, at:at + w]).then_inc(s_min[p % 2], DMA)

            def store_piece(p):
                w = PIECES[p] // QUARTERS * P
                act.wait_ge(s_ml, p + 1)
                act.dma_start(m_split[p, :, :, 0:w], m_parts[:, p % 2, :, 0:w]).then_inc(s_ms[p % 2], DMA)

            def place_piece(p):
                w = PIECES[p] // QUARTERS * P
                act.wait_ge(s_ms[p % 2], (p // 2 + 1) * DMA)
                for weights, row, part in ((pass1, 0, 0), (pass2, 0, 1), (pass1, 1, 0), (pass2, 1, 1),
                                           (pass1, 2, 0), (pass2, 2, 1), (pass1, 3, 2)):
                    dst = weights[D * row:D * (row + 1), PIECE_AT[p]:PIECE_AT[p + 1], :]
                    act.dma_start(dst.rearrange("d (q c) n -> d q (c n)", q=QUARTERS),
                                  m_split[p, :, part, 0:w].rearrange("(q d) n -> d q n", d=D)).then_inc(s_m[p], DMA)

            def split_piece(p):
                w = PIECES[p] // QUARTERS * P
                act.wait_ge(s_min[p % 2], (p // 2 + 1) * DMA)
                if p >= 2:
                    act.wait_ge(s_ms[p % 2], p // 2 * DMA)
                act.activation(m_parts[:, p % 2, 0, 0:w], m_in[:, p % 2, 0:w], ACT.Copy).then_inc(s_mh, 1)
                act.wait_ge(s_mr, p + 1)
                act.activation(m_parts[:, p % 2, 1, 0:w], m_in[:, p % 2, 0:w], ACT.Copy).then_inc(s_mm, 1)

            def pieces(u):
                for p, at in SPLIT_AT.items():
                    if u == at:
                        split_piece(p)
                    if u == at + 1:
                        store_piece(p)
                        if p + 1 < NP:
                            load_piece(p + 1)
                    if u == at + 3:
                        place_piece(p)

            def one_block(n, first, last):
                turns, lows = turns_in(first, last), lows_in(first, last)
                for u in range(NU):
                    if first:
                        pieces(u)
                    if u in lows and lows[u] != turns.get(u):
                        g, ahead = lows[u]
                        middle(n + ahead, g)
                    if u >= LAG:
                        for t in tiles_done(u - LAG):
                            save_z(n, t)
                    elif not first:
                        for t in tiles_done(NU + u - LAG):
                            save_z(n - 1, t)
                    if u in turns:
                        g, ahead = turns[u]
                        save_rows(n + ahead, g)
                        high(n + ahead, g)
                    if u in lows and lows[u] == turns.get(u):
                        g, ahead = lows[u]
                        middle(n + ahead, g)
                    if u in MLP_AT and not first:
                        save_h(n - 1, MLP_AT.index(u))

            load_piece(0)
            load_piece(1)
            split_piece(0)
            split_piece(1)
            store_piece(0)
            load_piece(2)
            store_piece(1)
            place_piece(0)
            save_rows(0, 0)
            high(0, 0)
            middle(0, 0)
            place_piece(1)
            one_block(0, True, False)
            act.wait_ge(s_w, 5 * DMA)
            with act.Fori(1, NB - 1) as n:
                one_block(n, False, False)
            one_block(NB - 1, False, True)
            save_z(NB - 1, ZT - 1)
            for j in range(HJ):
                save_h(NB - 1, j, tail_bank(j))

        @block.vector
        def _(dve):
            def left(n, g):
                dve.wait_ge(s_hi, n * NG + g + 1)
                dve.tensor_tensor(rest[:, g % 2, :], xcols[:, g, :], parts[:, g % 2, 0, :],
                                  ALU.subtract).then_inc(s_rest, 1)

            def low(n, g):
                dve.wait_ge(s_mid, n * NG + g + 1)
                dve.tensor_tensor(parts[:, g % 2, 2, :], rest[:, g % 2, :], parts[:, g % 2, 1, :],
                                  ALU.subtract).then_inc(s_parts, 1)

            def products(n, u):
                G, _, chunks = UNITS[u]
                k = len(chunks)
                dve.wait_ge(s_y, n * NU + u + 1)
                dve.wait_ge(s_cols, n * NG + G + 1)
                dve.tensor_tensor(prod[:, u % PRODS, 0:k, :], Y[u % 2][:, 0:k, :],
                                  xcols[:, G:G + 1, :].to_broadcast([P, k, BLK]), ALU.mult).then_inc(s_prod, 1)

            def pieces(ps):
                for p in ps:
                    w = PIECES[p] // QUARTERS * P
                    raw = m_in[:, p % 2, 0:w]
                    dve.wait_ge(s_mh, p + 1)
                    dve.tensor_tensor(raw, raw, m_parts[:, p % 2, 0, 0:w], ALU.subtract).then_inc(s_mr, 1)
                    dve.wait_ge(s_mm, p + 1)
                    dve.tensor_tensor(m_parts[:, p % 2, 2, 0:w], raw, m_parts[:, p % 2, 1, 0:w],
                                      ALU.subtract).then_inc(s_ml, 1)

            def one_block(n, first, last):
                lefts, lows = lefts_in(first, last), lows_in(first, last)
                for u in range(NU):
                    if first:
                        pieces([p for p in SPLIT_AT if SPLIT_AT[p] == u])
                    products(n, u)
                    if u in lows and lows[u] != lefts.get(u):
                        g, ahead = lows[u]
                        low(n + ahead, g)
                    if u in lefts:
                        g, ahead = lefts[u]
                        left(n + ahead, g)
                    if u in lows and lows[u] == lefts.get(u):
                        g, ahead = lows[u]
                        low(n + ahead, g)

            pieces((0, 1))
            left(0, 0)
            low(0, 0)
            one_block(0, True, False)
            with dve.Fori(1, NB - 1) as n:
                one_block(n, False, False)
            one_block(NB - 1, False, True)


def kernel(**inputs):
    import numpy as np
    import concourse.bacc as bacc
    from concourse.bass_utils import run_bass_kernel_spmd

    def pair(i, j):
        return i * (2 * FIELDS - i - 1) // 2 + j - i - 1

    bil = np.asarray(inputs["L0_rec_bilinear_matrices"])
    m_rows = np.zeros((D, CHUNKS, GF, D), bil.dtype)
    top1 = np.asarray(inputs["W_top1"])
    w1 = np.zeros((ZT * P, HID1), top1.dtype)
    for u, (G, _, chunks) in enumerate(UNITS):
        for k, chunk in enumerate(chunks):
            c = FIRST_CHUNK[u] + k
            tile, q, o, _, _ = place(c)
            for s0, s1, i in chunk:
                for s in range(s0, s1):
                    j = GF * G + s
                    if i is not None:
                        at = pair(min(i, j), max(i, j))
                        m_rows[:, c, s, :] = bil[at] if i < j else bil[at].T
                        w1[tile * P + 32 * q + GF * o + s] = top1[at]
    m_wide = np.concatenate([
        m_rows[:, a:b].reshape(D, QUARTERS, -1).transpose(1, 0, 2).reshape(P, -1)
        for a, b in zip(PIECE_AT, PIECE_AT[1:])], axis=1)
    pairs = FIELDS * (FIELDS - 1) // 2
    w1[ZT * P - DENSE:] = top1[pairs:]

    nc = bacc.Bacc("TRN2", target_bir_lowering=False, num_devices=1)
    arrays = {}

    def give(name, a):
        a = np.ascontiguousarray(a)
        arrays[name] = a
        return nc.dram_tensor(name, a.shape, mybir.dt.from_np(a.dtype), kind="ExternalInput").ap()

    args = [
        give("ids", inputs["ids"]), give("dense_ctx", inputs["dense_ctx"]),
        [give(f"tbl_{f}", inputs[f"tbl_{f}"]) for f in range(FIELDS)],
        give("m_wide", m_wide), give("w1", w1),
        give("b1", np.asarray(inputs["b_top1"]).reshape(H1T, P).T), give("w2", inputs["W_top2"]),
        give("b2", np.asarray(inputs["b_top2"]).reshape(H2T, P).T),
        give("w3", np.asarray(inputs["W_top3"]).reshape(H2T, P).T),
        nc.dram_tensor("out_0", (BATCH, 1), F32, kind="ExternalOutput").ap(),
    ]
    tower(nc, *args)
    r = run_bass_kernel_spmd(nc, [arrays], core_ids=[0])
    return r.results[0]["out_0"]
```
